# Optimizing a Trainium2 kernel written in Bass

```python
import numpy as np
import jax
import jax.numpy as jnp

def _softmax(x, axis=-1):
    return jax.nn.softmax(x, axis=axis)
def _gelu(x):
    return jax.nn.gelu(x, approximate=True)
def _silu(x):
    return jax.nn.silu(x)
def _sigmoid(x):
    return jax.nn.sigmoid(x)
def _layernorm(x, axis=-1, eps=1e-5):
    m = jnp.mean(x, axis=axis, keepdims=True)
    v = jnp.var(x, axis=axis, keepdims=True)
    return (x - m) / jnp.sqrt(v + eps)
def _scatter_add(tgt, idx, src, axis=0):
    return tgt.at[idx].add(src)
def _segment_sum(src, seg, n):
    return jax.ops.segment_sum(src, seg, n)

kernel_name = 'mk_conv_preact_d1_conv_nchw256_20b66c'

def setup_inputs(seed: int = 0):
    np.random.seed(seed)
    _w = jnp.asarray
    def _rec_inputs():
        import jax
        import jax.numpy as jnp
        _gk = jax.random.key(seed)
        x = -2.928e-05 + 0.1 * jax.random.normal(jax.random.fold_in(_gk, 1), (4, 256, 64, 64), jnp.float32)
        return x
    x = _rec_inputs()
    def _L0_conv_setup():
        import jax, jax.numpy as jnp
        import numpy as np
        B, C, H, W = (4, 256, 64, 64)
        CI = C // 2
        EPS = 1e-05
        key = jax.random.key(seed)
        ks = jax.random.split(key, 3)
        return {'x': jax.random.normal(ks[0], (B, C, H, W), dtype=jnp.float32) * 0.1, 'g_w': jax.random.normal(ks[1], (CI, C), dtype=jnp.float32) * 0.05, 'g_b': jnp.zeros((CI,), dtype=jnp.float32), 'W_w': jax.random.normal(ks[2], (C, CI), dtype=jnp.float32) * 0.05, 'W_b': jnp.zeros((C,), dtype=jnp.float32), 'gamma': jnp.ones((C,), dtype=jnp.float32), 'beta': jnp.zeros((C,), dtype=jnp.float32)}
    _L0_conv_all = _L0_conv_setup()
    _L0_conv_in = {k: v for k, v in _L0_conv_all.items() if k in ('g_w', 'g_b', 'W_w', 'W_b', 'gamma', 'beta', )}
    del _L0_conv_all

    return {
        "x": x,
        "L0_conv_g_w": _L0_conv_in["g_w"],
        "L0_conv_g_b": _L0_conv_in["g_b"],
        "L0_conv_W_w": _L0_conv_in["W_w"],
        "L0_conv_W_b": _L0_conv_in["W_b"],
        "L0_conv_gamma": _L0_conv_in["gamma"],
        "L0_conv_beta": _L0_conv_in["beta"],
    }

def reference(x, L0_conv_g_w, L0_conv_g_b, L0_conv_W_w, L0_conv_W_b, L0_conv_gamma, L0_conv_beta):
    import jax
    import jax.numpy as jnp
    def _L0_conv_ref(x, g_w, g_b, W_w, W_b, gamma, beta):
        import jax, jax.numpy as jnp
        import numpy as np
        B, C, H, W = (4, 256, 64, 64)
        CI = C // 2
        EPS = 1e-05
        b, c, h, w = x.shape
        n = h * w
        ci = g_w.shape[0]
        g_x = jnp.einsum('oc,bchw->bohw', g_w, x) + g_b[None, :, None, None]
        g_x = g_x.reshape(b, ci, n).transpose(0, 2, 1)
        theta = x.reshape(b, c, n).transpose(0, 2, 1)
        phi = x.reshape(b, c, n)
        f = jnp.einsum('bnc,bcm->bnm', theta, phi)
        attn = jax.nn.softmax(f, axis=-1)
        y = jnp.einsum('bnm,bmc->bnc', attn, g_x)
        y = y.transpose(0, 2, 1).reshape(b, ci, h, w)
        wy = jnp.einsum('oc,bchw->bohw', W_w, y) + W_b[None, :, None, None]
        mean = wy.mean(axis=(0, 2, 3))
        var = wy.var(axis=(0, 2, 3))
        wy = (wy - mean[None, :, None, None]) * jax.lax.rsqrt(var[None, :, None, None] + EPS)
        wy = wy * gamma[None, :, None, None] + beta[None, :, None, None]
        return wy + x

    def _gn(v, G=32, eps=1e-5):
        B_, C_, H_, W_ = v.shape
        g = v.reshape(B_, G, C_ // G, H_, W_)
        m = jnp.mean(g, axis=(2, 3, 4), keepdims=True)
        s = jnp.var(g, axis=(2, 3, 4), keepdims=True)
        return ((g - m) / jnp.sqrt(s + eps)).reshape(v.shape)

    def _ln_c(v, eps=1e-6):
        m = jnp.mean(v, axis=1, keepdims=True)
        s = jnp.var(v, axis=1, keepdims=True)
        return (v - m) / jnp.sqrt(s + eps)

    def _ln_t(v, eps=1e-5):
        m = jnp.mean(v, axis=-1, keepdims=True)
        s = jnp.var(v, axis=-1, keepdims=True)
        return (v - m) / jnp.sqrt(s + eps)

    def _to_tokens(v):
        B_, C_, H_, W_ = v.shape
        return v.reshape(B_, C_, H_ * W_).transpose(0, 2, 1)
    def _from_tokens(t, like):
        B_, C_, H_, W_ = like.shape
        return t.transpose(0, 2, 1).reshape(B_, C_, H_, W_)

    x = x + _L0_conv_ref(_gn(x), L0_conv_g_w, L0_conv_g_b, L0_conv_W_w, L0_conv_W_b, L0_conv_gamma, L0_conv_beta)
    return x


_drawn_inputs = setup_inputs


def setup_inputs(seed=0):
    import zlib

    import numpy as np

    out = dict(_drawn_inputs(seed))
    spreads = {'L0_conv_g_b': (0.0, 0.1),
     'L0_conv_W_b': (0.0, 0.1),
     'L0_conv_gamma': (1.0, 0.2),
     'L0_conv_beta': (0.0, 0.1)}
    factors = {}
    for name, (base, spread) in spreads.items():
        noise = np.random.default_rng([zlib.crc32(name.encode()), seed]).standard_normal(out[name].shape)
        drawn = base * np.exp(spread * noise) if base else spread * noise
        out[name] = jnp.asarray(drawn.astype(out[name].dtype))
    for name, factor in factors.items():
        out[name] = (out[name] * factor).astype(out[name].dtype)
    return out
```

```python
from contextlib import ExitStack

import concourse.bass as bass
from concourse import mybir

F32 = mybir.dt.float32
F32R = mybir.dt.float32r
ALU = mybir.AluOpType
ACT = mybir.ActivationFunctionType
AX = mybir.AxisListType

P = 128
B, C, N = 4, 256, 4096
CI = 128
K = C // P
W = 512
NB = N // W
T = W // P
TPB = NB * T
TILES = NB * TPB
GROUP = 8
GN_EPS, BN_EPS = 1e-5, 1e-5

SLOTS = 8
LBUFS = 5
HIS, LOS = 3, 2
LAG = 2


def pair(i, j):
    return i * NB - i * (i + 1) // 2 + (j - i - 1)


PAIRS = NB * (NB - 1) // 2
CHUNKS = [(j, c) for j in range(NB) for c in range(j, NB)]
CHUNK_NO = {jc: u for u, jc in enumerate(CHUNKS)}
PRODUCTS = [(j, c, t) for j, c in CHUNKS for t in range(T)]
PRODUCT_NO = {jct: s for s, jct in enumerate(PRODUCTS)}
NPROD = len(PRODUCTS)
NLEFT = PAIRS * T


def tile(p):
    j, i = divmod(p, TPB)
    c, r = divmod(i, T)
    return j, c, r, c < j


def left_no(p):
    j, i = divmod(p, TPB)
    return T * (j * (j - 1) // 2) + min(i, T * j)


def right_no(p):
    return p - left_no(p)


LEFT = [p for p in range(TILES) if tile(p)[3]]


def last_use(u):
    j, c = CHUNKS[u]
    return j * TPB + c * T + T - 1


def plan_products():
    at = {}
    for j in range(1, NB):
        n = T * (NB - j)
        for q in range(n):
            c, t = j + q // T, q % T
            u = CHUNK_NO[j, c]
            step = (j - 1) * TPB + q * 22 // n
            if u >= SLOTS:
                step = max(step, last_use(u - SLOTS) + 1 + t)
            at[j, c, t] = min(step, j * TPB - 1)
    return at


PRODUCT_STEP = plan_products()
PRODUCTS_AT = [[x for x in PRODUCTS if PRODUCT_STEP.get(x) == s] for s in range(TILES)]
MAX_STEP = {j: max(PRODUCT_STEP[x] for x in PRODUCTS if x[0] == j) for j in range(1, NB)}


def plan_exps():
    at = {}
    for j, c in CHUNKS:
        for t in range(T):
            at[j, c, t] = j * TPB + max(T * c - 7 + t, -LAG)
    return at


EXP_STEP = plan_exps()
EXPS_AT = {s: [x for x in PRODUCTS if EXP_STEP[x] == s] for s in range(-LAG, TILES)}
EXP_NO = {x: n for n, x in enumerate(x for s in range(-LAG, TILES) for x in EXPS_AT[s])}
LAST_EXP = {j: max(EXP_NO[x] for x in EXP_NO if x[0] == j) for j in range(NB)}

SPILLS = {k: [u for u, (j, c) in enumerate(CHUNKS) if c > j and u % SLOTS == k] for k in range(SLOTS)}
LOADS = {k: [w for w in range(NLEFT) if w % LBUFS == k] for k in range(LBUFS)}
LOAD_STEP = [max(LEFT[w] - 9, LEFT[w - LBUFS] - 1 if w >= LBUFS else 0) for w in range(NLEFT)]
SPILLS_AT = {}
for _u, (_j, _c) in enumerate(CHUNKS):
    if _c > _j:
        SPILLS_AT.setdefault(PRODUCT_STEP.get((_j, _c, T - 1), -1), []).append(_u)
WY_AT = (2, 6)


def plan_shared():
    order = []
    for s in range(TILES + 1):
        jj, i = divmod(s, TPB)
        for hh in range(K):
            if jj >= 1 and s < TILES and i == WY_AT[hh]:
                order.append(("wy", jj - 1, hh))
        if s < TILES and jj + 1 < NB and s == MAX_STEP[jj + 1]:
            order += [("cols", jj + 1, 0), ("rows", jj + 1, 0)]
    order += [("wy", NB - 1, hh) for hh in range(K)]
    return order


SHARED = plan_shared()


def nonlocal_block(nc, x, wg, bg, ww, vec, out):
    spill = nc.dram_tensor("spill", [PAIRS, P, T, W], F32, kind="Internal").ap()
    wyd = nc.dram_tensor("wyd", [B, K, P, N], F32, kind="Internal").ap()
    xd = x.rearrange("b (k p) n -> b p k n", p=P)
    outd = out.rearrange("b (k p) n -> b p k n", p=P)

    with ExitStack() as ctx:
        def sb(name, shape, dt=F32):
            return ctx.enter_context(nc.sbuf_tensor(name, shape, dt))

        def psum(name, shape):
            return ctx.enter_context(nc.psum_tensor(name, shape, F32))

        def sem(name):
            return ctx.enter_context(nc.semaphore(name))

        xh = sb("xh", [P, K, N], F32R)
        xl = sb("xl", [P, K, N], F32R)
        gh = sb("gh", [P, NB, T, CI], F32R)
        gl = sb("gl", [P, NB, T, CI], F32R)
        ring = sb("ring", [P, SLOTS, T, W])
        xraw = ring[:, SLOTS // 2:, :, :].rearrange("p s t w -> p (s t w)").rearrange("p (k n) -> p k n", k=K)
        wraw = ring[:, 0, 0, 0:K * CI].rearrange("p (k c) -> p k c", k=K)
        colmax = sb("colmax", [P, NB - 1, W])
        lbuf = sb("lbuf", [P, LBUFS, W])
        phi = sb("phi", [P, HIS, W], F32R)
        plo = sb("plo", [P, LOS, W], F32R)
        maxrow = sb("maxrow", [P, W])
        yn = sb("yn", [P, W])
        wys = sb("wys", [P, W])
        ident = sb("ident", [P, P])
        gavg = sb("gavg", [P, P])
        ones = sb("ones", [P, P], F32R)
        wgh = sb("wgh", [P, K, CI], F32R)
        wgl = sb("wgl", [P, K, CI], F32R)
        wwt = sb("wwt", [P, C])
        bgb = sb("bgb", [P, CI])
        vecs = sb("vecs", [P, 3, K])
        bst = sb("bst", [P, K, NB, 6])
        mv = sb("mv", [P, K, 2])
        gst = sb("gst", [P, 4, K])
        neghalf = sb("neghalf", [P, K])
        gnp = sb("gnp", [P, B, 2, K])
        rowm = sb("rowm", [P, T, NB])
        mx = sb("mx", [P, 2, T])
        rmax = sb("rmax", [P, 2, T])
        nmax = sb("nmax", [P, 2, T])
        rsum = sb("rsum", [P, 2, T, NB])
        lsum = sb("lsum", [P, T])
        bns = sb("bns", [P, K, B * NB, 6])
        bnmv = sb("bnmv", [P, K, 2])
        bnp = sb("bnp", [P, 3, K])
        shift = sb("shift", [P, B, K])

        fps = psum("fps", [P, 2, W])
        pps = psum("pps", [P, 2, W])
        yps = psum("yps", [P, 2, W])
        lps = psum("lps", [P, W])
        sps = psum("sps", [P, W])

        consts_in = sem("consts_in")
        consts_made = sem("consts_made")
        zeroed = sem("zeroed")
        dve_step = sem("dve_step")
        wg_hi = sem("wg_hi")
        x_in = sem("x_in")
        gn_in = sem("gn_in")
        gn_avg = sem("gn_avg")
        gn_var = sem("gn_var")
        gn_rstd = sem("gn_rstd")
        xn_made = sem("xn_made")
        xh_made = sem("xh_made")
        xl_made = sem("xl_made")
        g_made = sem("g_made")
        g_added = sem("g_added")
        gh_made = sem("gh_made")
        gl_made = sem("gl_made")
        f_made = sem("f_made")
        f_taken = sem("f_taken")
        cols_made = sem("cols_made")
        cols_taken = sem("cols_taken")
        max_made = sem("max_made")
        rows_made = sem("rows_made")
        maxrow_made = sem("maxrow_made")
        spilled = [sem(f"spilled{k}") for k in range(SLOTS)]
        loaded = [sem(f"loaded{k}") for k in range(LBUFS)]
        left_sub = sem("left_sub")
        left_exp = sem("left_exp")
        right_exp = sem("right_exp")
        turned = sem("turned")
        hi_made = sem("hi_made")
        lo_made = sem("lo_made")
        tile_used = sem("tile_used")
        lsum_made = sem("lsum_made")
        sums_made = sem("sums_made")
        sums_taken = sem("sums_taken")
        y_made = sem("y_made")
        wy_made = sem("wy_made")
        wy_taken = sem("wy_taken")
        wy_counted = sem("wy_counted")
        wy_out = sem("wy_out")
        images_done = sem("images_done")
        bn_var = sem("bn_var")
        bn_rstd = sem("bn_rstd")
        bn_ready = sem("bn_ready")
        fin_in = [sem(f"fin_in{k}") for k in range(4)]
        fin_scaled = sem("fin_scaled")
        fin_added = sem("fin_added")
        fin_out = [sem(f"fin_out{k}") for k in range(4)]

        FQ = 2
        FW = N // FQ
        PIECES = [(b, k, q) for b in range(B) for k in range(K) for q in range(FQ)]
        ringf = ring[:, :, :, :].rearrange("p s t w -> p s (t w)")

        block = ctx.enter_context(nc.Block())

        @block.sync
        def _(sp):
            sp.dma_start(wraw, wg.rearrange("(k p) c -> p k c", p=P)).then_inc(consts_in, 16)
            sp.dma_start(wwt[:, :], ww).then_inc(consts_in, 16)
            sp.dma_start(bgb[:, :], bg.partition_broadcast(P)).then_inc(consts_in, 16)
            sp.dma_start(vecs[:, :, :], vec).then_inc(consts_in, 16)
            with sp.Fori(0, B) as b:
                for k in range(K):
                    sp.dma_start(xraw[:, k, :], xd[bass.ds(b, 1), :, k, :].rearrange("b p n -> p (b n)")).then_inc(x_in, 16)
                sent = {k: 0 for k in range(SLOTS)}

                def send(u):
                    j, c = CHUNKS[u]
                    sp.wait_ge(f_taken, b * NPROD + PRODUCT_NO[j, c, T - 1] + 1)
                    sp.dma_start(spill[pair(j, c)], ring[:, u % SLOTS, :, :]).then_inc(spilled[u % SLOTS], 16)

                for u in SPILLS_AT.get(-1, []):
                    send(u)
                for s in range(TILES):
                    for w in range(NLEFT):
                        if LOAD_STEP[w] == s:
                            j, i, r, _ = tile(LEFT[w])
                            u = CHUNK_NO[i, j]
                            k = u % SLOTS
                            if w < LBUFS:
                                sp.wait_ge(spilled[k], b * (16 * len(SPILLS[k])) + 16 * (SPILLS[k].index(u) + 1))
                            else:
                                sp.wait_ge(left_exp, b * NLEFT + w - LBUFS + 1)
                            sp.dma_start(lbuf[:, w % LBUFS, :], spill[pair(i, j), :, r, :]
                                         ).then_inc(loaded[w % LBUFS], 16)
                    for u in SPILLS_AT.get(s, []):
                        send(u)
                    for h in range(K):
                        if s >= TPB and s % TPB == WY_AT[h] + 1:
                            j = s // TPB - 1
                            sp.wait_ge(wy_taken, b * (K * NB) + K * j + h + 1)
                            sp.dma_start(wyd[bass.ds(b, 1), h, :, j * W:(j + 1) * W].rearrange("b p w -> p (b w)"),
                                         wys[:, :]).then_inc(wy_out, 16)
                for h in range(K):
                    sp.wait_ge(wy_taken, b * (K * NB) + K * (NB - 1) + h + 1)
                    sp.dma_start(wyd[bass.ds(b, 1), h, :, (NB - 1) * W:].rearrange("b p w -> p (b w)"),
                                 wys[:, :]).then_inc(wy_out, 16)
                sp.wait_ge(wy_out, b * (16 * K * NB) + 16 * K * NB)
                sp.sem_inc(images_done, 1)
            for f in range(len(PIECES) + 2):
                if f < len(PIECES):
                    b, k, q = PIECES[f]
                    if f >= 4:
                        sp.wait_ge(fin_out[f % 4], 16 * (f // 4))
                    sp.dma_start(ringf[:, f % 4, :], xd[b, :, k, q * FW:(q + 1) * FW]).then_inc(fin_in[f % 4], 16)
                    sp.dma_start(ringf[:, 4 + f % 4, :], wyd[b, k, :, q * FW:(q + 1) * FW]).then_inc(fin_in[f % 4], 16)
                if f >= 2:
                    g = f - 2
                    b, k, q = PIECES[g]
                    sp.wait_ge(fin_added, g + 1)
                    sp.dma_start(outd[b, :, k, q * FW:(q + 1) * FW], ringf[:, g % 4, :]).then_inc(fin_out[g % 4], 16)
            for n in range(4):
                sp.wait_ge(fin_out[n], 16 * (len(PIECES) // 4))

        @block.gpsimd
        def _(pool):
            nc.gpsimd.memset(neghalf[:, :], -0.5)
            nc.gpsimd.memset(ones[:, :].bitcast(F32), 1.0)
            nc.gpsimd.memset(ident[:, :], 0.0)
            nc.gpsimd.memset(gavg[:, :], 1.0 / GROUP).then_inc(zeroed, 1)
            pool.wait_ge(zeroed, 1)
            nc.gpsimd.affine_select(out=ident[:, :], in_=ident[:, :], compare_op=ALU.not_equal, fill=1.0, base=0,
                                    pattern=[[-1, P]], channel_multiplier=1)
            gv = gavg[:, :].rearrange("p (g c) -> p g c", c=GROUP)
            nc.gpsimd.affine_select(out=gv, in_=gv, compare_op=ALU.is_ge, fill=0.0, base=0,
                                    pattern=[[-GROUP, P // GROUP], [0, GROUP]], channel_multiplier=1).then_inc(zeroed, 1)
            pool.wait_ge(zeroed, 2)
            nc.gpsimd.affine_select(out=gv, in_=gv, compare_op=ALU.is_ge, fill=0.0, base=GROUP - 1,
                                    pattern=[[GROUP, P // GROUP], [0, GROUP]], channel_multiplier=-1
                                    ).then_inc(consts_made, 1)
            with pool.Fori(0, B) as b:
                pool.wait_ge(gn_var, b + 1)
                nc.gpsimd.tensor_tensor(gst[:, 3, :], gst[:, 2, :], neghalf[:, :], ALU.pow).then_inc(gn_rstd, 1)
                for w in range(NLEFT):
                    j = tile(LEFT[w])[0]
                    k = w % LBUFS
                    if w == T * (j * (j - 1) // 2):
                        pool.wait_ge(maxrow_made, b * (NB - 1) + j)
                    pool.wait_ge(loaded[k], b * (16 * len(LOADS[k])) + 16 * (w // LBUFS + 1))
                    nc.gpsimd.tensor_tensor(lbuf[:, k, :], lbuf[:, k, :], maxrow[:, :], ALU.subtract).then_inc(left_sub, 1)
            pool.wait_ge(bn_var, 1)
            nc.gpsimd.tensor_tensor(bnp[:, 0, :], bnp[:, 0, :], neghalf[:, :], ALU.pow).then_inc(bn_rstd, 1)

        @block.scalar
        def _(act):
            act.wait_ge(consts_in, 16 * 4)
            nc.scalar.copy(wgh[:, :, :], wraw).then_inc(wg_hi, 1)
            with act.Fori(0, B) as b:
                def make_xh(c):
                    act.wait_ge(xn_made, b * NB + c + 1)
                    nc.scalar.copy(xh[:, :, c * W:(c + 1) * W], xraw[:, :, c * W:(c + 1) * W]).then_inc(xh_made, 1)

                def exp_right(j, c, t):
                    u = CHUNK_NO[j, c]
                    k = u % SLOTS
                    if t == 0:
                        act.wait_ge(max_made, b * NB + j + 1)
                        if c > j:
                            act.wait_ge(spilled[k], b * (16 * len(SPILLS[k])) + 16 * (SPILLS[k].index(u) + 1))
                    nc.scalar.activation(ring[:, k, t, :], ring[:, k, t, :], ACT.Exp, bias=nmax[:, j % 2, t:t + 1],
                                         accum_out=rsum[:, j % 2, t, c:c + 1]).then_inc(right_exp, 1)

                def take_wy(j, h):
                    n = K * j + h
                    act.wait_ge(wy_made, b * (K * NB) + n + 1)
                    if n > 0:
                        act.wait_ge(wy_out, b * (16 * K * NB) + 16 * n)
                        act.wait_ge(wy_counted, b * (K * NB) + n)
                    nc.scalar.activation(wys[:, :], sps[:, :], ACT.Identity, bias=vecs[:, 0, h:h + 1]
                                         ).then_inc(wy_taken, 1)

                make_xh(0)
                make_xh(1)
                for c in range(NB):
                    for cc in (2 * c + 2, 2 * c + 3):
                        if cc < NB:
                            make_xh(cc)
                    act.wait_ge(g_added, b * NB + c + 1)
                    nc.scalar.copy(gh[:, c, :, :], yn[:, :].rearrange("p (t c) -> p t c", t=T)).then_inc(gh_made, 1)
                for x3 in EXPS_AT[-LAG]:
                    exp_right(*x3)
                for s in range(-LAG, TILES):
                    p = s + LAG
                    if p < TILES:
                        j, c, r, left = tile(p)
                        if left:
                            w = left_no(p)
                            if c == 0 and r == 0:
                                act.wait_ge(rows_made, b * (NB - 1) + j)
                                if w > 0:
                                    act.wait_ge(left_sub, b * NLEFT + w)
                                nc.scalar.copy(maxrow[:, :], sps[:, :]).then_inc(maxrow_made, 1)
                            act.wait_ge(left_sub, b * NLEFT + w + 1)
                            act.wait_ge(lo_made, b * TILES + p - 1)
                            nc.scalar.activation(pps[:, p % 2, :], lbuf[:, w % LBUFS, :], ACT.Exp).then_inc(left_exp, 1)
                            act.wait_ge(left_exp, b * NLEFT + w + 1)
                        else:
                            act.wait_ge(turned, b * (TILES - NLEFT) + right_no(p) + 1)
                        if p >= HIS:
                            act.wait_ge(tile_used, b * TILES + p - HIS + 1)
                        nc.scalar.copy(phi[:, p % HIS, :], pps[:, p % 2, :]).then_inc(hi_made, 1)
                    if s > -LAG:
                        for x3 in EXPS_AT[s]:
                            exp_right(*x3)
                    for h in range(K):
                        if s >= TPB and s % TPB == WY_AT[h]:
                            take_wy(s // TPB - 1, h)
                for h in range(K):
                    take_wy(NB - 1, h)
            act.wait_ge(bn_ready, 1)
            for f, (b, k, q) in enumerate(PIECES):
                act.wait_ge(fin_in[f % 4], 32 * (f // 4 + 1))
                nc.scalar.activation(ringf[:, 4 + f % 4, :], ringf[:, 4 + f % 4, :], ACT.Identity,
                                     scale=bnp[:, 1, k:k + 1], bias=shift[:, b, k:k + 1]).then_inc(fin_scaled, 1)

        @block.vector
        def _(dve):
            dve.wait_ge(wg_hi, 1)
            nc.vector.tensor_tensor(wgl[:, :, :], wraw, wgh[:, :, :].bitcast(F32), ALU.subtract).then_inc(dve_step, 1)

            BEFORE = 1
            PER_IMAGE = 6 + 1 + 2 * (NB - 1)
            with dve.Fori(0, B) as b:
                count = [0]

                def own(ins):
                    count[0] += 1
                    ins.then_inc(dve_step, 1)
                    dve.wait_ge(dve_step, b * PER_IMAGE + BEFORE + count[0])

                dve.wait_ge(x_in, b * (16 * K) + 16 * K)
                for k in range(K):
                    for c in range(NB):
                        last = nc.vector.bn_stats(bst[:, k, c, :], xraw[:, k, c * W:(c + 1) * W])
                own(last)
                nc.vector.memset(gst[:, 3, :], 0.0)
                for k in range(K):
                    last = nc.vector.bn_aggr(mv[:, k, :], bst[:, k, :, :])
                last.then_inc(gn_in, 1)
                dve.wait_ge(gn_avg, b * 2 + 1)
                own(nc.vector.tensor_copy(gst[:, 0, :], sps[:, 0:K]))
                own(nc.vector.tensor_tensor(gst[:, 1, :], mv[:, :, 0], gst[:, 0, :], ALU.subtract))
                own(nc.vector.tensor_tensor(gst[:, 1, :], gst[:, 1, :], gst[:, 1, :], ALU.mult))
                nc.vector.tensor_tensor(gst[:, 1, :], gst[:, 1, :], mv[:, :, 1], ALU.add).then_inc(gn_in, 1)
                dve.wait_ge(gn_avg, b * 2 + 2)
                nc.vector.tensor_scalar(gst[:, 2, :], sps[:, K:2 * K], GN_EPS, None, ALU.add).then_inc(gn_var, 1)
                own(nc.vector.tensor_copy(gnp[:, bass.ds(b, 1), 0, :].rearrange("p b k -> p (b k)"), gst[:, 0, :]))
                dve.wait_ge(gn_rstd, b + 1)
                own(nc.vector.tensor_scalar(gnp[:, bass.ds(b, 1), 1, :].rearrange("p b k -> p (b k)"), gst[:, 3, :],
                                            1.0, None, ALU.add))

                def make_xn(c):
                    cols = slice(c * W, (c + 1) * W)
                    for k in range(K):
                        last = nc.vector.tensor_scalar(xraw[:, k, cols], xraw[:, k, cols], gst[:, 0, k:k + 1],
                                                       gst[:, 3, k:k + 1], ALU.subtract, ALU.mult)
                    last.then_inc(xn_made, 1)

                def make_xl(c):
                    cols = slice(c * W, (c + 1) * W)
                    dve.wait_ge(xh_made, b * NB + c + 1)
                    nc.vector.tensor_tensor(xl[:, :, cols], xraw[:, :, cols], xh[:, :, cols].bitcast(F32),
                                            ALU.subtract).then_inc(xl_made, 1)

                def take_f(j, c, t):
                    s = PRODUCT_NO[j, c, t]
                    u = CHUNK_NO[j, c]
                    if t == 0 and u >= SLOTS:
                        dve.wait_ge(tile_used, b * TILES + last_use(u - SLOTS) + 1)
                    dve.wait_ge(f_made, b * NPROD + s + 1)
                    src = fps[:, s % 2, :]
                    last = nc.vector.tensor_scalar(ring[:, u % SLOTS, t, :], src, 1.0, None, ALU.mult, ALU.max,
                                                   accum_out=rowm[:, t, c:c + 1])
                    if c > j:
                        cm = colmax[:, c - 1, :]
                        if j == 0 and t == 0:
                            last = nc.vector.tensor_copy(cm, src)
                        else:
                            if t > 0:
                                dve.wait_ge(f_taken, b * NPROD + s)
                            last = nc.vector.tensor_tensor(cm, src, cm, ALU.max)
                    last.then_inc(f_taken, 1)

                def merge_max(j):
                    own_max = rmax[:, j % 2, :]
                    dve.wait_ge(f_taken, b * NPROD + PRODUCT_NO[j, NB - 1, T - 1] + 1)
                    if j == 0:
                        own(nc.vector.tensor_reduce(own_max, rowm[:, :, j:], AX.X, ALU.max))
                    else:
                        nc.vector.tensor_reduce(mx[:, 0, :], rowm[:, :, j:], AX.X, ALU.max)
                        dve.wait_ge(cols_made, b * (NB - 1) + j)
                        own(nc.vector.tensor_reduce(mx[:, 1, :], sps[:, :].rearrange("p (t c) -> p t c", t=T),
                                                    AX.X, ALU.max))
                        own(nc.vector.tensor_tensor(own_max, mx[:, 0, :], mx[:, 1, :], ALU.max))
                    nc.vector.tensor_scalar(nmax[:, j % 2, :], own_max, -1.0, None, ALU.mult).then_inc(max_made, 1)

                def sum_right(j):
                    dve.wait_ge(right_exp, b * NPROD + LAST_EXP[j] + 1)
                    nc.vector.tensor_reduce(lsum[:, :], rsum[:, j % 2, :, j:], AX.X, ALU.add).then_inc(lsum_made, 1)

                def finish_y(j):
                    dve.wait_ge(sums_made, b * NB + j + 1)
                    nc.vector.reciprocal(yn[:, :], lps[:, :]).then_inc(sums_taken, 1)
                    dve.wait_ge(sums_taken, b * NB + j + 1)
                    nc.vector.tensor_tensor(yn[:, :], yps[:, j % 2, :], yn[:, :], ALU.mult).then_inc(y_made, 1)

                def count_wy(j, h):
                    dve.wait_ge(wy_taken, b * (K * NB) + K * j + h + 1)
                    nc.vector.bn_stats(bns[:, h, bass.ds(b * NB + j, 1), :].rearrange("p n s -> p (n s)"), wys[:, :]
                                       ).then_inc(wy_counted, 1)

                def lead_in(c):
                    make_xn(c)
                    make_xl(c)

                lead_in(0)
                lead_in(1)
                for c in range(NB):
                    for cc in (2 * c + 2, 2 * c + 3):
                        if cc < NB:
                            lead_in(cc)
                    for t in range(T):
                        take_f(0, c, t)
                    dve.wait_ge(g_made, b * NB + c + 1)
                    nc.vector.tensor_tensor(yn[:, :].rearrange("p (t c) -> p t c", t=T),
                                            pps[:, c % 2, :].rearrange("p (t c) -> p t c", t=T),
                                            bgb[:, :].unsqueeze(1).broadcast_to([P, T, CI]), ALU.add).then_inc(g_added, 1)
                    dve.wait_ge(gh_made, b * NB + c + 1)
                    nc.vector.tensor_tensor(gl[:, c, :, :], yn[:, :].rearrange("p (t c) -> p t c", t=T),
                                            gh[:, c, :, :].bitcast(F32), ALU.subtract).then_inc(gl_made, 1)
                merge_max(0)
                for p in range(TILES):
                    j, i = divmod(p, TPB)
                    dve.wait_ge(hi_made, b * TILES + p + 1)
                    if p >= LOS:
                        dve.wait_ge(tile_used, b * TILES + p - LOS + 1)
                    nc.vector.tensor_tensor(plo[:, p % LOS, :], pps[:, p % 2, :], phi[:, p % HIS, :].bitcast(F32),
                                            ALU.subtract).then_inc(lo_made, 1)
                    for x3 in PRODUCTS_AT[p]:
                        take_f(*x3)
                    if j + 1 < NB and p == MAX_STEP[j + 1]:
                        merge_max(j + 1)
                    for h in range(K):
                        if j >= 1 and i == WY_AT[h]:
                            count_wy(j - 1, h)
                    if i == TPB - 2:
                        sum_right(j)
                    if i == TPB - 1:
                        finish_y(j)
                for h in range(K):
                    count_wy(NB - 1, h)
                assert count[0] == PER_IMAGE
            dve.wait_ge(wy_counted, B * K * NB)
            end = [B * PER_IMAGE + BEFORE]

            def own_end(ins):
                end[0] += 1
                ins.then_inc(dve_step, 1)
                dve.wait_ge(dve_step, end[0])

            for k in range(K):
                last = nc.vector.bn_aggr(bnmv[:, k, :], bns[:, k, :, :])
            own_end(last)
            nc.vector.tensor_scalar(bnp[:, 0, :], bnmv[:, :, 1], BN_EPS, None, ALU.add).then_inc(bn_var, 1)
            dve.wait_ge(bn_rstd, 1)
            own_end(nc.vector.tensor_tensor(bnp[:, 1, :], bnp[:, 0, :], vecs[:, 1, :], ALU.mult))
            own_end(nc.vector.tensor_tensor(bnp[:, 2, :], bnmv[:, :, 0], bnp[:, 1, :], ALU.mult))
            own_end(nc.vector.tensor_tensor(bnp[:, 2, :], vecs[:, 2, :], bnp[:, 2, :], ALU.subtract))
            for b in range(B):
                last = nc.vector.tensor_tensor(shift[:, b, :], bnp[:, 2, :], gnp[:, b, 0, :], ALU.add)
            last.then_inc(bn_ready, 1)
            for f, (b, k, q) in enumerate(PIECES):
                dve.wait_ge(fin_in[f % 4], 32 * (f // 4 + 1))
                own_end(nc.vector.tensor_scalar(ringf[:, f % 4, :], ringf[:, f % 4, :], gnp[:, b, 0, k:k + 1],
                                                gnp[:, b, 1, k:k + 1], ALU.subtract, ALU.mult))
                dve.wait_ge(fin_scaled, f + 1)
                nc.vector.tensor_tensor(ringf[:, f % 4, :], ringf[:, f % 4, :], ringf[:, 4 + f % 4, :],
                                        ALU.add).then_inc(fin_added, 1)

        @block.tensor
        def _(pe):
            pe.wait_ge(consts_made, 1)
            pe.wait_ge(dve_step, 1)
            with pe.Fori(0, B) as b:
                pe.wait_ge(gn_in, b * 2 + 1)
                nc.tensor.matmul(sps[:, 0:K], gavg[:, :], mv[:, :, 0], start=True, stop=True).then_inc(gn_avg, 1)
                pe.wait_ge(gn_in, b * 2 + 2)
                nc.tensor.matmul(sps[:, K:2 * K], gavg[:, :], gst[:, 1, :], start=True, stop=True).then_inc(gn_avg, 1)

                def multiply(j, c, t):
                    s = PRODUCT_NO[j, c, t]
                    if s >= 2:
                        pe.wait_ge(f_taken, b * NPROD + s - 1)
                    rows = slice(j * W + t * P, j * W + (t + 1) * P)
                    cols = slice(c * W, (c + 1) * W)
                    dst = fps[:, s % 2, :]
                    for k in range(K):
                        nc.tensor.matmul(dst, xh[:, k, rows], xh[:, k, cols], start=(k == 0), stop=False)
                        nc.tensor.matmul(dst, xh[:, k, rows], xl[:, k, cols], start=False, stop=False)
                        last = nc.tensor.matmul(dst, xl[:, k, rows], xh[:, k, cols], start=False, stop=(k == K - 1))
                    last.then_inc(f_made, 1)

                def turn(p):
                    j, c, r, left = tile(p)
                    if left:
                        return
                    pe.wait_ge(right_exp, b * NPROD + max(EXP_NO[j, c, t] for t in range(T)) + 1)
                    if p >= 2:
                        pe.wait_ge(lo_made, b * TILES + p - 1)
                    k = CHUNK_NO[j, c] % SLOTS
                    for t in range(T):
                        last = nc.tensor.transpose(pps[:, p % 2, t * P:(t + 1) * P],
                                                   ring[:, k, t, r * P:(r + 1) * P], ident[:, :])
                    last.then_inc(turned, 1)

                def attend(p):
                    j, c, r, left = tile(p)
                    i = p % TPB
                    pe.wait_ge(lo_made, b * TILES + p + 1)
                    hi, lo = phi[:, p % HIS, :], plo[:, p % LOS, :]
                    y = yps[:, j % 2, :]
                    if i == 0 and j >= 2:
                        pe.wait_ge(y_made, b * NB + j - 1)
                    nc.tensor.matmul(y, gh[:, c, r, :], hi, start=(i == 0), stop=False)
                    nc.tensor.matmul(y, gl[:, c, r, :], hi, start=False, stop=False)
                    last = nc.tensor.matmul(y, gh[:, c, r, :], lo, start=False, stop=(i == TPB - 1))
                    if left:
                        if i == 0:
                            pe.wait_ge(sums_taken, b * NB + j)
                        nc.tensor.matmul(lps[:, :], ones[:, :], hi, start=(i == 0), stop=False)
                        last = nc.tensor.matmul(lps[:, :], ones[:, :], lo, start=False, stop=(i == T * j - 1))
                    last.then_inc(tile_used, 1)

                def shared_free(kind, j, h=0):
                    n = SHARED.index((kind, j, h))
                    if n == 0:
                        return
                    pk, pj, ph = SHARED[n - 1]
                    if pk == "cols":
                        pe.wait_ge(max_made, b * NB + pj + 1)
                    elif pk == "rows":
                        pe.wait_ge(maxrow_made, b * (NB - 1) + pj)
                    else:
                        pe.wait_ge(wy_taken, b * (K * NB) + K * pj + ph + 1)

                def spread_max(j):
                    shared_free("cols", j)
                    pe.wait_ge(f_taken, b * NPROD + PRODUCT_NO[j - 1, j, T - 1] + 1)
                    for t in range(T):
                        last = nc.tensor.transpose(sps[:, t * P:(t + 1) * P], colmax[:, j - 1, t * P:(t + 1) * P],
                                                   ident[:, :])
                    last.then_inc(cols_made, 1)
                    shared_free("rows", j)
                    for t in range(T):
                        last = nc.tensor.matmul(sps[:, t * P:(t + 1) * P],
                                                rmax[:, j % 2, t:t + 1].broadcast_to([P, P]), ident[:, :],
                                                start=True, stop=True)
                    last.then_inc(rows_made, 1)

                def spread_sums(j):
                    pe.wait_ge(lsum_made, b * NB + j + 1)
                    for t in range(T):
                        last = nc.tensor.matmul(lps[:, t * P:(t + 1) * P], lsum[:, t:t + 1].broadcast_to([P, P]),
                                                ident[:, :], start=(j == 0), stop=True,
                                                skip_group_check=True)
                    last.then_inc(sums_made, 1)

                def project(j, h):
                    pe.wait_ge(y_made, b * NB + j + 1)
                    shared_free("wy", j, h)
                    nc.tensor.matmul(sps[:, :], wwt[:, h * P:(h + 1) * P], yn[:, :], start=True, stop=True
                                     ).then_inc(wy_made, 1)

                for c in range(NB):
                    pe.wait_ge(xl_made, b * NB + c + 1)
                    for t in range(T):
                        multiply(0, c, t)
                    if c >= 2:
                        pe.wait_ge(g_added, b * NB + c - 1)
                    for r in range(T):
                        rows = slice(c * W + r * P, c * W + (r + 1) * P)
                        dst = pps[:, c % 2, r * CI:(r + 1) * CI]
                        for k in range(K):
                            nc.tensor.matmul(dst, xh[:, k, rows], wgh[:, k, :], start=(k == 0), stop=False)
                            nc.tensor.matmul(dst, xh[:, k, rows], wgl[:, k, :], start=False, stop=False)
                            last = nc.tensor.matmul(dst, xl[:, k, rows], wgh[:, k, :], start=False, stop=(k == K - 1))
                    last.then_inc(g_made, 1)
                pe.wait_ge(gl_made, b * NB + NB)
                for p in range(LAG):
                    turn(p)
                for p in range(TILES):
                    j, i = divmod(p, TPB)
                    if p + LAG < TILES:
                        turn(p + LAG)
                    for x3 in PRODUCTS_AT[p]:
                        multiply(*x3)
                    attend(p)
                    if i == TPB - 1:
                        spread_sums(j)
                    for h in range(K):
                        if j >= 1 and i == WY_AT[h]:
                            project(j - 1, h)
                    if j + 1 < NB and p == MAX_STEP[j + 1]:
                        spread_max(j + 1)
                for h in range(K):
                    project(NB - 1, h)


_INS = ("x", "wg", "bg", "ww", "vec")


def kernel(x, L0_conv_g_w, L0_conv_g_b, L0_conv_W_w, L0_conv_W_b, L0_conv_gamma, L0_conv_beta):
    import numpy as np
    import concourse.bacc as bacc
    from concourse.bass_utils import run_bass_kernel_spmd

    nc = bacc.Bacc("TRN2", target_bir_lowering=False, num_devices=1)
    shape = np.shape(x)
    given = dict(
        x=np.ascontiguousarray(x).reshape(B, C, N),
        wg=np.ascontiguousarray(np.transpose(L0_conv_g_w)),
        bg=np.ascontiguousarray(L0_conv_g_b),
        ww=np.ascontiguousarray(np.transpose(L0_conv_W_w)),
        vec=np.ascontiguousarray(np.transpose(np.reshape(
            np.stack([L0_conv_W_b, L0_conv_gamma, L0_conv_beta]), (3, K, P)), (2, 0, 1))),
    )
    args = [nc.dram_tensor(f"{n}_dram", given[n].shape, F32, kind="ExternalInput").ap() for n in _INS]
    out = nc.dram_tensor("out_dram", (B, C, N), F32, kind="ExternalOutput").ap()
    nonlocal_block(nc, *args, out)
    r = run_bass_kernel_spmd(nc, [{f"{n}_dram": given[n] for n in _INS}], core_ids=[0])
    return r.results[0]["out_dram"].reshape(shape)
```

```python
from contextlib import ExitStack

import concourse.bass as bass
from concourse import mybir

F32 = mybir.dt.float32
F32R = mybir.dt.float32r
ALU = mybir.AluOpType
ACT = mybir.ActivationFunctionType
AX = mybir.AxisListType

P = 128
B, C, N = 4, 256, 4096
CI = 128
K = C // P
W = 512
NB = N // W
T = W // P
TPB = NB * T
TILES = NB * TPB
GROUP = 8
GN_EPS, BN_EPS = 1e-5, 1e-5

SLOTS = 8
LBUFS = 4
HIS, LOS = 3, 2
LAG = 2


def pair(i, j):
    return i * NB - i * (i + 1) // 2 + (j - i - 1)


PAIRS = NB * (NB - 1) // 2
CHUNKS = [(j, c) for j in range(NB) for c in range(j, NB)]
CHUNK_NO = {jc: u for u, jc in enumerate(CHUNKS)}
PRODUCTS = [(j, c, t) for j, c in CHUNKS for t in range(T)]
PRODUCT_NO = {jct: s for s, jct in enumerate(PRODUCTS)}
NPROD = len(PRODUCTS)
NLEFT = PAIRS * T


def plan_order(j):
    right = [((c - j) / (NB - j), c) for c in range(j, NB)]
    left = [((c + (0.5 if j > 1 else -0.5)) / j, c) for c in range(j)]
    return [c for _, c in sorted(right + left)]


ORDER = [plan_order(j) for j in range(NB)]


def tile(p):
    j, i = divmod(p, TPB)
    c = ORDER[j][i // T]
    return j, c, i % T, c < j


LEFT = [p for p in range(TILES) if tile(p)[3]]
RIGHT = [p for p in range(TILES) if not tile(p)[3]]
LEFT_NO = {p: w for w, p in enumerate(LEFT)}
RIGHT_NO = {p: n for n, p in enumerate(RIGHT)}
LEFT_OF = {j: [w for w, p in enumerate(LEFT) if p // TPB == j] for j in range(1, NB)}


def last_use(u):
    j, c = CHUNKS[u]
    return j * TPB + ORDER[j].index(c) * T + T - 1


def plan_products():
    at = {}
    for j in range(1, NB):
        n = T * (NB - j)
        for q in range(n):
            c, t = j + q // T, q % T
            u = CHUNK_NO[j, c]
            step = (j - 1) * TPB + q * 22 // n
            if u >= SLOTS:
                step = max(step, last_use(u - SLOTS) + 1 + t)
            at[j, c, t] = min(step, j * TPB - 1)
    return at


PRODUCT_STEP = plan_products()
PRODUCTS_AT = [[x for x in PRODUCTS if PRODUCT_STEP.get(x) == s] for s in range(TILES)]
TAKE_STEP = {x: min(s + 1, x[0] * TPB - 1) for x, s in PRODUCT_STEP.items()}
TAKES_AT = [[x for x in PRODUCTS if TAKE_STEP.get(x) == s] for s in range(TILES)]
COLS_STEP = {j: max(TAKE_STEP[x] for x in PRODUCTS if x[0] == j) for j in range(1, NB)}
ROWS_STEP = {j: min(COLS_STEP[j] + 1, j * TPB - 1) for j in range(1, NB)}


def plan_exps():
    at = {}
    for j, c in CHUNKS:
        merged = COLS_STEP[j] + 1 if j else -LAG
        for t in range(T):
            step = j * TPB + T * ORDER[j].index(c) - 7 + t
            at[j, c, t] = max(step, min(merged, j * TPB - LAG))
    return at


EXP_STEP = plan_exps()
EXPS_AT = {s: [x for x in PRODUCTS if EXP_STEP[x] == s] for s in range(-LAG, TILES)}
EXP_NO = {x: n for n, x in enumerate(x for s in range(-LAG, TILES) for x in EXPS_AT[s])}
LAST_EXP = {j: max(EXP_NO[x] for x in EXP_NO if x[0] == j) for j in range(NB)}

SPILLS = {k: [u for u, (j, c) in enumerate(CHUNKS) if c > j and u % SLOTS == k] for k in range(SLOTS)}
LOADS = {k: [w for w in range(NLEFT) if w % LBUFS == k] for k in range(LBUFS)}
LOAD_STEP = [max(LEFT[w] - 9, LEFT[w - LBUFS] - 1 if w >= LBUFS else 0) for w in range(NLEFT)]
SPILLS_AT = {}
for _u, (_j, _c) in enumerate(CHUNKS):
    if _c > _j:
        SPILLS_AT.setdefault(TAKE_STEP.get((_j, _c, T - 1), -1), []).append(_u)
INVERT_AT, TAKE_AT, SCALE_AT, WY_AT = 0, 1, 3, (5, 9)
G_AT = {T * (c - 1) - 1: c for c in range(2, NB)}
MAXROW_AT = {min(max(ROWS_STEP[j], LEFT[LEFT_OF[j - 1][-1]] - 1 if j > 1 else 0), LEFT[LEFT_OF[j][0]] - LAG): j
             for j in range(1, NB)}
X_AT = (NB - 2) * TPB
STATS_AT = X_AT + 10
GROUP_AT = STATS_AT + NB
XN_AT = GROUP_AT + 4
NEXT_AT = XN_AT + 4
NEXT_PRODUCTS = {NEXT_AT + q: x for q, x in enumerate(PRODUCTS[:T * NB])}
assert max(NEXT_PRODUCTS) < TILES - 1
LAST_IN_SLOT = {k: max(u for u in range(len(CHUNKS)) if u % SLOTS == k) for k in range(SLOTS)}
AHEAD = {s: min(w for w, p in enumerate(LEFT) if p > s + 3) for s in range(GROUP_AT + 2, XN_AT + NB)}
FQ = 2
FW = N // FQ
PIECES = [(b, k, q) for b in range(B) for k in range(K) for q in range(FQ)]
FBUFS = SLOTS // 2


def plan_shared():
    order = [("g", 0, 0), ("g", 0, 1)]
    for s in range(TILES):
        jj, i = divmod(s, TPB)
        if s in G_AT:
            order.append(("g", 0, G_AT[s]))
        if jj >= 1 and i in WY_AT:
            order.append(("wy", jj - 1, WY_AT.index(i)))
        if jj + 1 < NB and s == COLS_STEP[jj + 1]:
            order.append(("cols", jj + 1, 0))
        if jj + 1 < NB and s == ROWS_STEP[jj + 1]:
            order.append(("rows", jj + 1, 0))
    order += [("wy", NB - 1, hh) for hh in range(K)]
    return order


SHARED = plan_shared()


def nonlocal_block(nc, x, wg, bg, ww, vec, out):
    spill = nc.dram_tensor("spill", [PAIRS, P, T, W], F32, kind="Internal").ap()
    wyd = nc.dram_tensor("wyd", [B, K, P, N], F32, kind="Internal").ap()
    xd = x.rearrange("b (k p) n -> b p k n", p=P)
    outd = out.rearrange("b (k p) n -> b p k n", p=P)

    with ExitStack() as ctx:
        def sb(name, shape, dt=F32):
            return ctx.enter_context(nc.sbuf_tensor(name, shape, dt))

        def psum(name, shape):
            return ctx.enter_context(nc.psum_tensor(name, shape, F32))

        def sem(name):
            return ctx.enter_context(nc.semaphore(name))

        xh = sb("xh", [P, K, N], F32R)
        xl = sb("xl", [P, K, N], F32R)
        gh = sb("gh", [P, NB, T, CI], F32R)
        gl = sb("gl", [P, NB, T, CI], F32R)
        ring = sb("ring", [P, SLOTS, T, W])
        ringf = ring[:, :, :, :].rearrange("p s t w -> p s (t w)")
        xraw = ring[:, SLOTS // 2:, :, :].rearrange("p s t w -> p (s t w)").rearrange("p (k n) -> p k n", k=K)
        wraw = ring[:, 0, 0, 0:K * CI].rearrange("p (k c) -> p k c", k=K)
        colmax = sb("colmax", [P, NB - 1, W])
        lbuf = sb("lbuf", [P, LBUFS, W])
        phi = sb("phi", [P, HIS, W], F32R)
        plo = sb("plo", [P, LOS, W], F32R)
        lacc = sb("lacc", [P, W])
        maxrow = sb("maxrow", [P, W])
        yn = sb("yn", [P, W])
        wys = sb("wys", [P, W])
        ident = sb("ident", [P, P])
        gavg = sb("gavg", [P, P])
        ones = sb("ones", [P, 2])
        wgh = sb("wgh", [P, K, CI], F32R)
        wgl = sb("wgl", [P, K, CI], F32R)
        wwt = sb("wwt", [P, C])
        bgb = sb("bgb", [P, CI])
        vecs = sb("vecs", [P, 3, K])
        bst = sb("bst", [P, K, NB, 6])
        mv = sb("mv", [P, K, 2])
        gst = sb("gst", [P, 4, K])
        neghalf = sb("neghalf", [P, K])
        gnp = sb("gnp", [P, B, 2, K])
        rowm = sb("rowm", [P, T, NB])
        mx = sb("mx", [P, 2, T])
        rmax = sb("rmax", [P, 2, T])
        nmax = sb("nmax", [P, 2, T])
        rsum = sb("rsum", [P, 2, T, NB])
        lsum = sb("lsum", [P, T])
        linv = sb("linv", [P, T])
        bns = sb("bns", [P, K, B * NB, 6])
        bnmv = sb("bnmv", [P, K, 2])
        bnp = sb("bnp", [P, 3, K])
        shift = sb("shift", [P, B, K])

        fps = psum("fps", [P, 2, W])
        pps = psum("pps", [P, 2, W])
        yps = psum("yps", [P, 2, W])
        lps = psum("lps", [P, W])
        sps = psum("sps", [P, W])

        consts_in = sem("consts_in")
        consts_made = sem("consts_made")
        zeroed = sem("zeroed")
        wg_hi = sem("wg_hi")
        wg_lo = sem("wg_lo")
        x_in = [sem(f"x_in{k}") for k in range(K)]
        counted = sem("counted")
        gn_own = sem("gn_own")
        gn_in = sem("gn_in")
        gn_avg = sem("gn_avg")
        gn_var = sem("gn_var")
        gn_rstd = sem("gn_rstd")
        gnp_made = sem("gnp_made")
        xn_made = sem("xn_made")
        xh_made = sem("xh_made")
        xl_made = sem("xl_made")
        g_made = sem("g_made")
        g_added = sem("g_added")
        gh_made = sem("gh_made")
        gl_made = sem("gl_made")
        f_made = sem("f_made")
        f_taken = sem("f_taken")
        cols_made = sem("cols_made")
        max_own = sem("max_own")
        max_made = sem("max_made")
        rows_made = sem("rows_made")
        maxrow_made = sem("maxrow_made")
        spilled = [sem(f"spilled{k}") for k in range(SLOTS)]
        loaded = [sem(f"loaded{k}") for k in range(LBUFS)]
        left_sub = sem("left_sub")
        left_exp = sem("left_exp")
        right_exp = sem("right_exp")
        turned = sem("turned")
        hi_made = sem("hi_made")
        lo_made = sem("lo_made")
        left_added = sem("left_added")
        tile_used = sem("tile_used")
        right_summed = sem("right_summed")
        left_summed = sem("left_summed")
        summed = sem("summed")
        inverted = sem("inverted")
        inverse_spread = sem("inverse_spread")
        inverse_taken = sem("inverse_taken")
        y_made = sem("y_made")
        wy_made = sem("wy_made")
        wy_taken = sem("wy_taken")
        wy_counted = sem("wy_counted")
        wy_free = sem("wy_free")
        bn_own = sem("bn_own")
        bn_var = sem("bn_var")
        bn_rstd = sem("bn_rstd")
        bn_ready = sem("bn_ready")
        fin_x = [sem(f"fin_x{k}") for k in range(FBUFS)]
        fin_wy = [sem(f"fin_wy{k}") for k in range(FBUFS)]
        fin_scaled = sem("fin_scaled")
        fin_own = sem("fin_own")
        fin_added = sem("fin_added")
        fin_out = [sem(f"fin_out{k}") for k in range(FBUFS)]

        block = ctx.enter_context(nc.Block())

        def spill_count(n, u):
            mine = SPILLS[u % SLOTS]
            return n * (16 * len(mine)) + 16 * (mine.index(u) + 1)

        def wait_bank(eng, b, p):
            if tile(p)[3]:
                eng.wait_ge(left_added, b * NLEFT + LEFT_NO[p] + 1)
            else:
                eng.wait_ge(lo_made, b * TILES + p + 1)

        @block.sync
        def _(sp):
            def load_x(n, k):
                sp.dma_start(xraw[:, k, :], xd[bass.ds(n, 1), :, k, :].rearrange("b p n -> p (b n)")
                             ).then_inc(x_in[k], 16)

            def send(n, u):
                sp.wait_ge(f_taken, n * NPROD + PRODUCT_NO[(*CHUNKS[u], T - 1)] + 1)
                sp.dma_start(spill[pair(*CHUNKS[u])], ring[:, u % SLOTS, :, :]).then_inc(spilled[u % SLOTS], 16)

            def load_left(b, w):
                j, i, r, _ = tile(LEFT[w])
                if w < LBUFS:
                    sp.wait_ge(spilled[CHUNK_NO[i, j] % SLOTS], spill_count(b, CHUNK_NO[i, j]))
                else:
                    sp.wait_ge(left_exp, b * NLEFT + w - LBUFS + 1)
                sp.dma_start(lbuf[:, w % LBUFS, :], spill[pair(i, j), :, r, :]).then_inc(loaded[w % LBUFS], 16)

            def store_wy(b, j, h):
                sp.wait_ge(wy_taken, b * (K * NB) + K * j + h + 1)
                sp.dma_start(wyd[bass.ds(b, 1), h, :, j * W:(j + 1) * W].rearrange("b p w -> p (b w)"),
                             wys[:, :]).then_inc(wy_free, 16)

            def load_final_x(f):
                b, k, q = PIECES[f]
                sp.dma_start(ringf[:, FBUFS + f % FBUFS, :], xd[b, :, k, q * FW:(q + 1) * FW]
                             ).then_inc(fin_x[f % FBUFS], 16)

            def image(b, more):
                for s in range(TILES):
                    if s == X_AT:
                        sp.wait_ge(tile_used, b * TILES + last_use(LAST_IN_SLOT[SLOTS - 1]) + 1)
                        if more:
                            for k in range(K):
                                load_x(b + 1, k)
                        else:
                            for f in range(FBUFS):
                                load_final_x(f)
                    for w in range(NLEFT):
                        if LOAD_STEP[w] == s:
                            load_left(b, w)
                    for u in SPILLS_AT.get(s, []):
                        send(b, u)
                    if more and s - 1 in NEXT_PRODUCTS:
                        j, c, t = NEXT_PRODUCTS[s - 1]
                        if c > j and t == T - 1:
                            send(b + 1, CHUNK_NO[j, c])
                    if s > TPB and s % TPB - 1 in WY_AT:
                        store_wy(b, s // TPB - 1, WY_AT.index(s % TPB - 1))
                for h in range(K):
                    store_wy(b, NB - 1, h)

            for k in range(K):
                load_x(0, k)
            sp.dma_start(wraw, wg.rearrange("(k p) c -> p k c", p=P)).then_inc(consts_in, 16)
            sp.dma_start(wwt[:, :], ww).then_inc(consts_in, 16)
            sp.dma_start(bgb[:, :], bg.partition_broadcast(P)).then_inc(consts_in, 16)
            sp.dma_start(vecs[:, :, :], vec).then_inc(wy_free, 16)
            for u in SPILLS_AT[-1]:
                send(0, u)
            with sp.Fori(0, B - 1) as b:
                image(b, True)
            image(B - 1, False)
            sp.wait_ge(wy_free, 16 * (B * K * NB + 1))
            for f in range(len(PIECES) + 2):
                if f < len(PIECES):
                    b, k, q = PIECES[f]
                    if f >= FBUFS:
                        sp.wait_ge(fin_out[f % FBUFS], 16 * (f // FBUFS))
                        load_final_x(f)
                    sp.dma_start(ringf[:, f % FBUFS, :], wyd[b, k, :, q * FW:(q + 1) * FW]
                                 ).then_inc(fin_wy[f % FBUFS], 16)
                if f >= 2:
                    g = f - 2
                    b, k, q = PIECES[g]
                    sp.wait_ge(fin_added, g + 1)
                    sp.dma_start(outd[b, :, k, q * FW:(q + 1) * FW], ringf[:, FBUFS + g % FBUFS, :]
                                 ).then_inc(fin_out[g % FBUFS], 16)
            for n in range(FBUFS):
                sp.wait_ge(fin_out[n], 16 * (len(PIECES) // FBUFS))

        @block.gpsimd
        def _(pool):
            def rstd(n):
                pool.wait_ge(gn_var, n + 1)
                nc.gpsimd.tensor_tensor(gst[:, 3, :], gst[:, 2, :], neghalf[:, :], ALU.pow).then_inc(gn_rstd, 1)

            def make_xl(n, c):
                cols = slice(c * W, (c + 1) * W)
                pool.wait_ge(xh_made, n * NB + c + 1)
                nc.gpsimd.tensor_tensor(xl[:, :, cols], xraw[:, :, cols], xh[:, :, cols].bitcast(F32),
                                        ALU.subtract).then_inc(xl_made, 1)

            def image(b, more):
                for c in range(NB):
                    pool.wait_ge(gh_made, b * NB + c + 1)
                    nc.gpsimd.tensor_tensor(gl[:, c, :, :], yn[:, :].rearrange("p (t c) -> p t c", t=T),
                                            gh[:, c, :, :].bitcast(F32), ALU.subtract).then_inc(gl_made, 1)
                for w in range(NLEFT):
                    if more and w == AHEAD[GROUP_AT + 2]:
                        rstd(b + 1)
                    for c in range(NB):
                        if more and w == AHEAD[XN_AT + c]:
                            make_xl(b + 1, c)
                    j = tile(LEFT[w])[0]
                    if w == LEFT_OF[j][0]:
                        pool.wait_ge(maxrow_made, b * (NB - 1) + j)
                    pool.wait_ge(loaded[w % LBUFS], b * (16 * len(LOADS[w % LBUFS])) + 16 * (w // LBUFS + 1))
                    nc.gpsimd.tensor_tensor(lbuf[:, w % LBUFS, :], lbuf[:, w % LBUFS, :], maxrow[:, :],
                                            ALU.subtract).then_inc(left_sub, 1)

            nc.gpsimd.memset(neghalf[:, :], -0.5)
            nc.gpsimd.memset(ones[:, :], 1.0)
            nc.gpsimd.memset(ident[:, :], 0.0)
            nc.gpsimd.memset(gavg[:, :], 1.0 / GROUP).then_inc(zeroed, 1)
            pool.wait_ge(zeroed, 1)
            nc.gpsimd.affine_select(out=ident[:, :], in_=ident[:, :], compare_op=ALU.not_equal, fill=1.0, base=0,
                                    pattern=[[-1, P]], channel_multiplier=1)
            gv = gavg[:, :].rearrange("p (g c) -> p g c", c=GROUP)
            nc.gpsimd.affine_select(out=gv, in_=gv, compare_op=ALU.is_ge, fill=0.0, base=0,
                                    pattern=[[-GROUP, P // GROUP], [0, GROUP]], channel_multiplier=1).then_inc(zeroed, 1)
            pool.wait_ge(zeroed, 2)
            nc.gpsimd.affine_select(out=gv, in_=gv, compare_op=ALU.is_ge, fill=0.0, base=GROUP - 1,
                                    pattern=[[GROUP, P // GROUP], [0, GROUP]], channel_multiplier=-1
                                    ).then_inc(consts_made, 1)
            rstd(0)
            for c in range(NB):
                make_xl(0, c)
            with pool.Fori(0, B - 1) as b:
                image(b, True)
            image(B - 1, False)
            pool.wait_ge(bn_var, 1)
            nc.gpsimd.tensor_tensor(bnp[:, 0, :], bnp[:, 0, :], neghalf[:, :], ALU.pow).then_inc(bn_rstd, 1)

        @block.scalar
        def _(act):
            def make_xh(n, c):
                act.wait_ge(xn_made, n * NB + c + 1)
                nc.scalar.copy(xh[:, :, c * W:(c + 1) * W], xraw[:, :, c * W:(c + 1) * W]).then_inc(xh_made, 1)

            def make_gh(b, c):
                act.wait_ge(g_added, b * NB + c + 1)
                nc.scalar.copy(gh[:, c, :, :], yn[:, :].rearrange("p (t c) -> p t c", t=T)).then_inc(gh_made, 1)

            def exp_right(b, j, c, t):
                u = CHUNK_NO[j, c]
                if t == 0:
                    act.wait_ge(max_made, b * NB + j + 1)
                    if c > j:
                        act.wait_ge(spilled[u % SLOTS], spill_count(b, u))
                nc.scalar.activation(ring[:, u % SLOTS, t, :], ring[:, u % SLOTS, t, :], ACT.Exp,
                                     bias=nmax[:, j % 2, t:t + 1], accum_out=rsum[:, j % 2, t, c:c + 1]
                                     ).then_inc(right_exp, 1)

            def take_maxrow(b, j):
                act.wait_ge(rows_made, b * (NB - 1) + j)
                if j > 1:
                    act.wait_ge(left_sub, b * NLEFT + LEFT_OF[j][0])
                nc.scalar.copy(maxrow[:, :], sps[:, :]).then_inc(maxrow_made, 1)

            def split_hi(b, p):
                if tile(p)[3]:
                    w = LEFT_NO[p]
                    act.wait_ge(left_sub, b * NLEFT + w + 1)
                    wait_bank(act, b, p - 2)
                    nc.scalar.activation(pps[:, p % 2, :], lbuf[:, w % LBUFS, :], ACT.Exp).then_inc(left_exp, 1)
                    act.wait_ge(left_exp, b * NLEFT + w + 1)
                else:
                    act.wait_ge(turned, b * (TILES - NLEFT) + RIGHT_NO[p] + 1)
                if p >= HIS:
                    act.wait_ge(tile_used, b * TILES + p - HIS + 1)
                nc.scalar.copy(phi[:, p % HIS, :], pps[:, p % 2, :]).then_inc(hi_made, 1)

            def take_inverse(b, j):
                act.wait_ge(inverse_spread, b * NB + j + 1)
                if j == 0:
                    act.wait_ge(gl_made, b * NB + NB)
                nc.scalar.copy(yn[:, :], lps[:, :]).then_inc(inverse_taken, 1)

            def take_wy(b, j, h):
                n = K * j + h
                act.wait_ge(wy_made, b * (K * NB) + n + 1)
                act.wait_ge(wy_free, b * (16 * K * NB) + 16 * (n + 1))
                if n > 0:
                    act.wait_ge(wy_counted, b * (K * NB) + n)
                nc.scalar.activation(wys[:, :], sps[:, :], ACT.Identity, bias=vecs[:, 0, h:h + 1]
                                     ).then_inc(wy_taken, 1)

            def image(b, more):
                for c in range(2):
                    make_gh(b, c)
                for x3 in EXPS_AT[-LAG]:
                    exp_right(b, *x3)
                for s in range(-LAG, TILES):
                    j, i = divmod(s, TPB)
                    if s in MAXROW_AT:
                        take_maxrow(b, MAXROW_AT[s])
                    if s + LAG < TILES:
                        split_hi(b, s + LAG)
                    if s > -LAG:
                        for x3 in EXPS_AT[s]:
                            exp_right(b, *x3)
                    if s - 1 in G_AT:
                        make_gh(b, G_AT[s - 1])
                    if j >= 1 and i == TAKE_AT:
                        take_inverse(b, j - 1)
                    if j >= 1 and i in WY_AT:
                        take_wy(b, j - 1, WY_AT.index(i))
                    if more and 0 <= s - XN_AT < NB:
                        make_xh(b + 1, s - XN_AT)
                take_inverse(b, NB - 1)
                for h in range(K):
                    take_wy(b, NB - 1, h)

            act.wait_ge(consts_in, 16 * 3)
            nc.scalar.copy(wgh[:, :, :], wraw).then_inc(wg_hi, 1)
            for c in range(NB):
                make_xh(0, c)
            with act.Fori(0, B - 1) as b:
                image(b, True)
            image(B - 1, False)
            act.wait_ge(bn_ready, 1)
            for f, (b, k, q) in enumerate(PIECES):
                act.wait_ge(fin_wy[f % FBUFS], 16 * (f // FBUFS + 1))
                nc.scalar.activation(ringf[:, f % FBUFS, :], ringf[:, f % FBUFS, :], ACT.Identity,
                                     scale=bnp[:, 1, k:k + 1], bias=shift[:, b, k:k + 1]).then_inc(fin_scaled, 1)

        @block.vector
        def _(dve):
            def count_x(n, i):
                k, c = divmod(2 * i, NB)
                if c == 0:
                    dve.wait_ge(x_in[k], n * 16 + 16)
                for cc in (c, c + 1):
                    last = nc.vector.bn_stats(bst[:, k, cc, :], xraw[:, k, cc * W:(cc + 1) * W])
                last.then_inc(counted, 1)

            def group(n, stage):
                if stage == 0:
                    dve.wait_ge(counted, n * NB + NB)
                    nc.vector.memset(gst[:, 3, :], 0.0)
                    for k in range(K):
                        last = nc.vector.bn_aggr(mv[:, k, :], bst[:, k, :, :])
                    last.then_inc(gn_in, 1)
                elif stage == 1:
                    dve.wait_ge(gn_avg, n * 2 + 1)
                    nc.vector.tensor_copy(gst[:, 0, :], lps[:, 0:K]).then_inc(gn_own, 1)
                    dve.wait_ge(gn_own, n * 3 + 1)
                    nc.vector.tensor_tensor(gst[:, 1, :], mv[:, :, 0], gst[:, 0, :], ALU.subtract).then_inc(gn_own, 1)
                    dve.wait_ge(gn_own, n * 3 + 2)
                    nc.vector.tensor_tensor(gst[:, 1, :], gst[:, 1, :], gst[:, 1, :], ALU.mult).then_inc(gn_own, 1)
                    dve.wait_ge(gn_own, n * 3 + 3)
                    nc.vector.tensor_tensor(gst[:, 1, :], gst[:, 1, :], mv[:, :, 1], ALU.add).then_inc(gn_in, 1)
                elif stage == 2:
                    dve.wait_ge(gn_avg, n * 2 + 2)
                    nc.vector.tensor_scalar(gst[:, 2, :], lps[:, K:2 * K], GN_EPS, None, ALU.add).then_inc(gn_var, 1)
                else:
                    nc.vector.tensor_copy(gnp[:, bass.ds(n, 1), 0, :].rearrange("p b k -> p (b k)"), gst[:, 0, :])
                    dve.wait_ge(gn_rstd, n + 1)
                    nc.vector.tensor_scalar(gnp[:, bass.ds(n, 1), 1, :].rearrange("p b k -> p (b k)"), gst[:, 3, :],
                                            1.0, None, ALU.add).then_inc(gnp_made, 1)

            def make_xn(n, c):
                cols = slice(c * W, (c + 1) * W)
                for k in range(K):
                    last = nc.vector.tensor_scalar(xraw[:, k, cols], xraw[:, k, cols], gst[:, 0, k:k + 1],
                                                   gst[:, 3, k:k + 1], ALU.subtract, ALU.mult)
                last.then_inc(xn_made, 1)

            def add_bias(b, c):
                dve.wait_ge(g_made, b * NB + c + 1)
                if c > 0:
                    dve.wait_ge(gl_made, b * NB + c)
                nc.vector.tensor_tensor(yn[:, :].rearrange("p (t c) -> p t c", t=T),
                                        sps[:, :].rearrange("p (t c) -> p t c", t=T),
                                        bgb[:, :].unsqueeze(1).broadcast_to([P, T, CI]), ALU.add).then_inc(g_added, 1)

            def take_f(n, j, c, t, before=True):
                s = PRODUCT_NO[j, c, t]
                u = CHUNK_NO[j, c]
                if t == 0:
                    if u >= SLOTS:
                        dve.wait_ge(tile_used, n * TILES + last_use(u - SLOTS) + 1)
                    else:
                        if before:
                            dve.wait_ge(tile_used, n * TILES + last_use(LAST_IN_SLOT[u]) + 1 - TILES)
                        if u >= SLOTS // 2:
                            dve.wait_ge(xl_made, n * NB + NB)
                dve.wait_ge(f_made, n * NPROD + s + 1)
                src = fps[:, s % 2, :]
                last = nc.vector.tensor_scalar(ring[:, u % SLOTS, t, :], src, 1.0, None, ALU.mult, ALU.max,
                                               accum_out=rowm[:, t, c:c + 1])
                if c > j:
                    cm = colmax[:, c - 1, :]
                    if j == 0 and t == 0:
                        last = nc.vector.tensor_copy(cm, src)
                    else:
                        if t > 0:
                            dve.wait_ge(f_taken, n * NPROD + s)
                        last = nc.vector.tensor_tensor(cm, src, cm, ALU.max)
                last.then_inc(f_taken, 1)

            def merge_max(n, j):
                own_max = rmax[:, j % 2, :]
                steps = n * (2 * NB - 1)
                dve.wait_ge(f_taken, n * NPROD + PRODUCT_NO[j, NB - 1, T - 1] + 1)
                if j == 0:
                    nc.vector.tensor_reduce(own_max, rowm[:, :, j:], AX.X, ALU.max).then_inc(max_own, 1)
                    dve.wait_ge(max_own, steps + 1)
                else:
                    nc.vector.tensor_reduce(mx[:, 0, :], rowm[:, :, j:], AX.X, ALU.max)
                    dve.wait_ge(cols_made, n * (NB - 1) + j)
                    nc.vector.tensor_reduce(mx[:, 1, :], sps[:, :].rearrange("p (t c) -> p t c", t=T),
                                            AX.X, ALU.max).then_inc(max_own, 1)
                    dve.wait_ge(max_own, steps + 2 * j)
                    nc.vector.tensor_tensor(own_max, mx[:, 0, :], mx[:, 1, :], ALU.max).then_inc(max_own, 1)
                    dve.wait_ge(max_own, steps + 2 * j + 1)
                nc.vector.tensor_scalar(nmax[:, j % 2, :], own_max, -1.0, None, ALU.mult).then_inc(max_made, 1)

            def split_lo(b, p):
                dve.wait_ge(hi_made, b * TILES + p + 1)
                if p >= LOS:
                    dve.wait_ge(tile_used, b * TILES + p - LOS + 1)
                last = nc.vector.tensor_tensor(plo[:, p % LOS, :], pps[:, p % 2, :], phi[:, p % HIS, :].bitcast(F32),
                                               ALU.subtract)
                last.then_inc(lo_made, 1)
                if tile(p)[3]:
                    w = LEFT_NO[p]
                    if w == LEFT_OF[p // TPB][0]:
                        nc.vector.tensor_copy(lacc[:, :], pps[:, p % 2, :]).then_inc(left_added, 1)
                    else:
                        dve.wait_ge(left_added, b * NLEFT + w)
                        nc.vector.tensor_tensor(lacc[:, :], pps[:, p % 2, :], lacc[:, :], ALU.add
                                                ).then_inc(left_added, 1)

            def sum_right(b, j):
                dve.wait_ge(right_exp, b * NPROD + LAST_EXP[j] + 1)
                nc.vector.tensor_reduce(lsum[:, :], rsum[:, j % 2, :, j:], AX.X, ALU.add).then_inc(right_summed, 1)

            def invert(b, j):
                dve.wait_ge(right_summed, b * NB + j + 1)
                if j > 0:
                    dve.wait_ge(left_summed, b * (NB - 1) + j)
                    nc.vector.tensor_tensor(lsum[:, :], lps[:, 0:2 * T].rearrange("p (t o) -> p t o", o=2)[:, :, 0],
                                            lsum[:, :], ALU.add).then_inc(summed, 1)
                    dve.wait_ge(summed, b * (NB - 1) + j)
                nc.vector.reciprocal(linv[:, :], lsum[:, :]).then_inc(inverted, 1)

            def scale(b, j):
                dve.wait_ge(inverse_taken, b * NB + j + 1)
                nc.vector.tensor_tensor(yn[:, :], yps[:, j % 2, :], yn[:, :], ALU.mult).then_inc(y_made, 1)

            def count_wy(b, j, h):
                dve.wait_ge(wy_taken, b * (K * NB) + K * j + h + 1)
                nc.vector.bn_stats(bns[:, h, bass.ds(b * NB + j, 1), :].rearrange("p n s -> p (n s)"), wys[:, :]
                                   ).then_inc(wy_counted, 1)

            def image(b, more):
                for c in range(2):
                    add_bias(b, c)
                for p in range(TILES):
                    j, i = divmod(p, TPB)
                    split_lo(b, p)
                    if p - 1 in G_AT:
                        add_bias(b, G_AT[p - 1])
                    if j >= 1 and i == INVERT_AT:
                        invert(b, j - 1)
                    for x3 in TAKES_AT[p]:
                        take_f(b, *x3)
                    if j + 1 < NB and p == COLS_STEP[j + 1]:
                        merge_max(b, j + 1)
                    if j >= 1 and i == SCALE_AT:
                        scale(b, j - 1)
                    if j >= 1 and i - 1 in WY_AT:
                        count_wy(b, j - 1, WY_AT.index(i - 1))
                    if more and 0 <= p - STATS_AT < NB:
                        count_x(b + 1, p - STATS_AT)
                    if more and 0 <= p - GROUP_AT < 4:
                        group(b + 1, p - GROUP_AT)
                    if more and 0 <= p - XN_AT < NB:
                        make_xn(b + 1, p - XN_AT)
                    if more and p - 1 in NEXT_PRODUCTS:
                        take_f(b + 1, *NEXT_PRODUCTS[p - 1])
                    if i == TPB - 2:
                        sum_right(b, j)
                if more:
                    merge_max(b + 1, 0)
                invert(b, NB - 1)
                scale(b, NB - 1)
                for h in range(K):
                    count_wy(b, NB - 1, h)

            dve.wait_ge(wg_hi, 1)
            nc.vector.tensor_tensor(wgl[:, :, :], wraw, wgh[:, :, :].bitcast(F32), ALU.subtract).then_inc(wg_lo, 1)
            for i in range(NB):
                count_x(0, i)
            for stage in range(4):
                group(0, stage)
            for c in range(NB):
                make_xn(0, c)
            for x3 in PRODUCTS[:T * NB]:
                take_f(0, *x3, before=False)
            merge_max(0, 0)
            with dve.Fori(0, B - 1) as b:
                image(b, True)
            image(B - 1, False)
            dve.wait_ge(wy_counted, B * K * NB)
            for k in range(K):
                last = nc.vector.bn_aggr(bnmv[:, k, :], bns[:, k, :, :])
            last.then_inc(bn_own, 1)
            dve.wait_ge(bn_own, 1)
            nc.vector.tensor_scalar(bnp[:, 0, :], bnmv[:, :, 1], BN_EPS, None, ALU.add).then_inc(bn_var, 1)
            dve.wait_ge(bn_rstd, 1)
            nc.vector.tensor_tensor(bnp[:, 1, :], bnp[:, 0, :], vecs[:, 1, :], ALU.mult).then_inc(bn_own, 1)
            dve.wait_ge(bn_own, 2)
            nc.vector.tensor_tensor(bnp[:, 2, :], bnmv[:, :, 0], bnp[:, 1, :], ALU.mult).then_inc(bn_own, 1)
            dve.wait_ge(bn_own, 3)
            nc.vector.tensor_tensor(bnp[:, 2, :], vecs[:, 2, :], bnp[:, 2, :], ALU.subtract).then_inc(bn_own, 1)
            dve.wait_ge(bn_own, 4)
            for b in range(B):
                last = nc.vector.tensor_tensor(shift[:, b, :], bnp[:, 2, :], gnp[:, b, 0, :], ALU.add)
            last.then_inc(bn_ready, 1)
            for f, (b, k, q) in enumerate(PIECES):
                px, pw = ringf[:, FBUFS + f % FBUFS, :], ringf[:, f % FBUFS, :]
                dve.wait_ge(fin_x[f % FBUFS], 16 * (f // FBUFS + 1))
                nc.vector.tensor_scalar(px, px, gnp[:, b, 0, k:k + 1], gnp[:, b, 1, k:k + 1],
                                        ALU.subtract, ALU.mult).then_inc(fin_own, 1)
                dve.wait_ge(fin_own, f + 1)
                dve.wait_ge(fin_scaled, f + 1)
                nc.vector.tensor_tensor(px, px, pw, ALU.add).then_inc(fin_added, 1)

        @block.tensor
        def _(pe):
            def average(n, stage, first=False):
                if stage == 0 and not first:
                    pe.wait_ge(inverse_taken, (n - 1) * NB + NB - 2)
                pe.wait_ge(gn_in, n * 2 + stage + 1)
                nc.tensor.matmul(lps[:, K * stage:K * (stage + 1)], gavg[:, :], gst[:, 1, :] if stage else mv[:, :, 0],
                                 start=True, stop=True).then_inc(gn_avg, 1)

            def multiply(n, j, c, t, first=False):
                s = PRODUCT_NO[j, c, t]
                if j == 0 and t == 0:
                    pe.wait_ge(xl_made, n * NB + c + 1)
                if s >= 2 or not first:
                    pe.wait_ge(f_taken, n * NPROD + s - 1)
                rows = slice(j * W + t * P, j * W + (t + 1) * P)
                cols = slice(c * W, (c + 1) * W)
                dst = fps[:, s % 2, :]
                for k in range(K):
                    nc.tensor.matmul(dst, xh[:, k, rows], xh[:, k, cols], start=(k == 0), stop=False)
                    nc.tensor.matmul(dst, xh[:, k, rows], xl[:, k, cols], start=False, stop=False)
                    last = nc.tensor.matmul(dst, xl[:, k, rows], xh[:, k, cols], start=False, stop=(k == K - 1))
                last.then_inc(f_made, 1)

            def make_g(b, c):
                shared_free(b, "g", 0, c)
                for r in range(T):
                    rows = slice(c * W + r * P, c * W + (r + 1) * P)
                    dst = sps[:, r * CI:(r + 1) * CI]
                    for k in range(K):
                        nc.tensor.matmul(dst, xh[:, k, rows], wgh[:, k, :], start=(k == 0), stop=False)
                        nc.tensor.matmul(dst, xh[:, k, rows], wgl[:, k, :], start=False, stop=False)
                        last = nc.tensor.matmul(dst, xl[:, k, rows], wgh[:, k, :], start=False, stop=(k == K - 1))
                last.then_inc(g_made, 1)

            def turn(b, p):
                j, c, r, left = tile(p)
                if left:
                    return
                pe.wait_ge(right_exp, b * NPROD + max(EXP_NO[j, c, t] for t in range(T)) + 1)
                if p >= 2:
                    wait_bank(pe, b, p - 2)
                k = CHUNK_NO[j, c] % SLOTS
                for t in range(T):
                    last = nc.tensor.transpose(pps[:, p % 2, t * P:(t + 1) * P],
                                               ring[:, k, t, r * P:(r + 1) * P], ident[:, :])
                last.then_inc(turned, 1)

            def attend(b, p):
                j, c, r, left = tile(p)
                i = p % TPB
                y = yps[:, j % 2, :]
                if j == 0 and r == 0:
                    pe.wait_ge(gl_made, b * NB + c + 1)
                pe.wait_ge(lo_made, b * TILES + p + 1)
                if i == 0 and j >= 2:
                    pe.wait_ge(y_made, b * NB + j - 1)
                hi, lo = phi[:, p % HIS, :], plo[:, p % LOS, :]
                nc.tensor.matmul(y, gh[:, c, r, :], hi, start=(i == 0), stop=False)
                nc.tensor.matmul(y, gl[:, c, r, :], hi, start=False, stop=False)
                nc.tensor.matmul(y, gh[:, c, r, :], lo, start=False, stop=(i == TPB - 1)).then_inc(tile_used, 1)

            def shared_free(b, kind, j, h=0):
                n = SHARED.index((kind, j, h))
                if n == 0:
                    return
                kind, j, h = SHARED[n - 1]
                if kind == "g":
                    pe.wait_ge(g_added, b * NB + h + 1)
                elif kind == "cols":
                    pe.wait_ge(max_made, b * NB + j + 1)
                elif kind == "rows":
                    pe.wait_ge(maxrow_made, b * (NB - 1) + j)
                else:
                    pe.wait_ge(wy_taken, b * (K * NB) + K * j + h + 1)

            def turn_cols(b, j):
                shared_free(b, "cols", j)
                pe.wait_ge(f_taken, b * NPROD + PRODUCT_NO[j - 1, j, T - 1] + 1)
                for t in range(T):
                    last = nc.tensor.transpose(sps[:, t * P:(t + 1) * P], colmax[:, j - 1, t * P:(t + 1) * P],
                                               ident[:, :])
                last.then_inc(cols_made, 1)

            def spread_rows(b, j):
                shared_free(b, "rows", j)
                for t in range(T):
                    last = nc.tensor.matmul(sps[:, t * P:(t + 1) * P], rmax[:, j % 2, t:t + 1].broadcast_to([P, P]),
                                            ident[:, :], start=True, stop=True)
                last.then_inc(rows_made, 1)

            def sum_left(b, j, more):
                pe.wait_ge(left_added, b * NLEFT + LEFT_OF[j][-1] + 1)
                pe.wait_ge(inverse_taken, b * NB + j)
                if more and j == NB - 2:
                    pe.wait_ge(gn_var, b + 2)
                for t in range(T):
                    last = nc.tensor.matmul(lps[:, 2 * t:2 * t + 2], lacc[:, t * P:(t + 1) * P], ones[:, :],
                                            start=True, stop=True)
                last.then_inc(left_summed, 1)

            def spread_inverse(b, j):
                pe.wait_ge(inverted, b * NB + j + 1)
                for t in range(T):
                    last = nc.tensor.matmul(lps[:, t * P:(t + 1) * P], linv[:, t:t + 1].broadcast_to([P, P]),
                                            ident[:, :], start=True, stop=True)
                last.then_inc(inverse_spread, 1)

            def project(b, j, h):
                pe.wait_ge(y_made, b * NB + j + 1)
                shared_free(b, "wy", j, h)
                nc.tensor.matmul(sps[:, :], wwt[:, h * P:(h + 1) * P], yn[:, :], start=True, stop=True
                                 ).then_inc(wy_made, 1)

            def image(b, more):
                for c in range(2):
                    make_g(b, c)
                for p in range(LAG):
                    turn(b, p)
                for p in range(TILES):
                    j, i = divmod(p, TPB)
                    if p + LAG < TILES:
                        turn(b, p + LAG)
                    for x3 in PRODUCTS_AT[p]:
                        multiply(b, *x3)
                    if more and p in NEXT_PRODUCTS:
                        multiply(b + 1, *NEXT_PRODUCTS[p])
                    attend(b, p)
                    if j > 0 and i == TPB - 1:
                        sum_left(b, j, more)
                    if j >= 1 and i == INVERT_AT:
                        spread_inverse(b, j - 1)
                    if p in G_AT:
                        make_g(b, G_AT[p])
                    if j >= 1 and i in WY_AT:
                        project(b, j - 1, WY_AT.index(i))
                    if j + 1 < NB and p == COLS_STEP[j + 1]:
                        turn_cols(b, j + 1)
                    if j + 1 < NB and p == ROWS_STEP[j + 1]:
                        spread_rows(b, j + 1)
                    if more and p - GROUP_AT in (0, 1):
                        average(b + 1, p - GROUP_AT)
                spread_inverse(b, NB - 1)
                for h in range(K):
                    project(b, NB - 1, h)
                pe.wait_ge(wy_taken, b * (K * NB) + K * NB)

            pe.wait_ge(consts_made, 1)
            pe.wait_ge(wg_lo, 1)
            for stage in range(2):
                average(0, stage, first=True)
            for x3 in PRODUCTS[:T * NB]:
                multiply(0, *x3, first=True)
            with pe.Fori(0, B - 1) as b:
                image(b, True)
            image(B - 1, False)


_INS = ("x", "wg", "bg", "ww", "vec")


def kernel(x, L0_conv_g_w, L0_conv_g_b, L0_conv_W_w, L0_conv_W_b, L0_conv_gamma, L0_conv_beta):
    import numpy as np
    import concourse.bacc as bacc
    from concourse.bass_utils import run_bass_kernel_spmd

    nc = bacc.Bacc("TRN2", target_bir_lowering=False, num_devices=1)
    shape = np.shape(x)
    given = dict(
        x=np.ascontiguousarray(x).reshape(B, C, N),
        wg=np.ascontiguousarray(np.transpose(L0_conv_g_w)),
        bg=np.ascontiguousarray(L0_conv_g_b),
        ww=np.ascontiguousarray(np.transpose(L0_conv_W_w)),
        vec=np.ascontiguousarray(np.transpose(np.reshape(
            np.stack([L0_conv_W_b, L0_conv_gamma, L0_conv_beta]), (3, K, P)), (2, 0, 1))),
    )
    args = [nc.dram_tensor(f"{n}_dram", given[n].shape, F32, kind="ExternalInput").ap() for n in _INS]
    out = nc.dram_tensor("out_dram", (B, C, N), F32, kind="ExternalOutput").ap()
    nonlocal_block(nc, *args, out)
    r = run_bass_kernel_spmd(nc, [{f"{n}_dram": given[n] for n in _INS}], core_ids=[0])
    return r.results[0]["out_dram"].reshape(shape)
```

```python
from contextlib import ExitStack

import concourse.bass as bass
from concourse import mybir

F32 = mybir.dt.float32
F32R = mybir.dt.float32r
ALU = mybir.AluOpType
ACT = mybir.ActivationFunctionType
AX = mybir.AxisListType

P = 128
B, C, N = 4, 256, 4096
CI = 128
K = C // P
W = 512
NB = N // W
T = W // P
TPB = NB * T
TILES = NB * TPB
X_CUTS = 2
GROUP = 8
GN_EPS, BN_EPS = 1e-5, 1e-5

SLOTS = 8
LBUFS = 5
HIS, LOS = 3, 2
LAG = 2
HEAD = 12


def pair(i, j):
    return i * NB - i * (i + 1) // 2 + (j - i - 1)


PAIRS = NB * (NB - 1) // 2
CHUNKS = [(j, c) for j in range(NB) for c in range(j, NB)]
CHUNK_NO = {jc: u for u, jc in enumerate(CHUNKS)}
SLOT = [0, 1, 2, 3, 4, 5, 6, 7,
        0, 1, 2, 3, 4, 5, 6,
        7, 0, 1, 2, 3, 4,
        5, 6, 7, 0, 1,
        2, 3, 4, 5,
        6, 7, 1,
        3, 2,
        3]
BEFORE = {u: max((v for v in range(u) if SLOT[v] == SLOT[u]), default=None) for u in range(len(CHUNKS))}
PRODUCTS = [(j, c, t) for j, c in CHUNKS for t in range(T)]
PRODUCT_NO = {jct: s for s, jct in enumerate(PRODUCTS)}
NPROD = len(PRODUCTS)


def turned_self(j, c):
    return c == j and 0 < j < NB - 1


def plan_tiles(j):
    first = j + 1 if turned_self(j, j) else j
    nr, nl = T * (NB - first), T * j
    if j == NB - 1:
        at = [0.04 * q for q in range(nr)]
    elif j == NB - 2:
        at = [0, 0.9, 0.95, 1]
    else:
        at = [q / (nr - 1) for q in range(nr)]
    right = [(at[q], first + q // T, q % T) for q in range(nr)]
    left = [(0.06 + 0.84 * (q + 0.5) / nl, q // T, q % T) for q in range(nl)]
    if first > j:
        left += [((0.13 if j == 1 else 0.07) + 0.035 * q, j, q) for q in range(T)]
    return [(c, r) for _, c, r in sorted(right + left)]


ORDER = [plan_tiles(j) for j in range(NB)]


def tile(p):
    j, i = divmod(p, TPB)
    c, r = ORDER[j][i]
    return j, c, r, c < j or turned_self(j, c)


LEFT = [p for p in range(TILES) if tile(p)[3]]
NLEFT = len(LEFT)
RIGHT = [p for p in range(TILES) if not tile(p)[3]]
LEFT_NO = {p: w for w, p in enumerate(LEFT)}
RIGHT_NO = {p: n for n, p in enumerate(RIGHT)}
LEFT_OF = {j: [w for w, p in enumerate(LEFT) if p // TPB == j] for j in range(1, NB)}
PE_SUMS = (NB - 2, NB - 1)
ADDED = [w for w, p in enumerate(LEFT) if p // TPB not in PE_SUMS]
NADD = len(ADDED)
HI_BUF = [p % HIS for p in range(TILES - 1)] + [1]
HI_BEFORE = [max(q for q in range(p - 2 * HIS, p) if HI_BUF[q % TILES] == HI_BUF[p]) for p in range(TILES)]
ADDS_AT = [[w for w in ADDED if min(LEFT[w] + 1, (LEFT[w] // TPB + 1) * TPB - 1) == p] for p in range(TILES)]
IN_PSUM = [p for p in range(TILES) if not tile(p)[3] or p // TPB in PE_SUMS]
PSUM_NO = {p: n for n, p in enumerate(IN_PSUM)}


def last_use(u):
    j, c = CHUNKS[u]
    return j * TPB + ORDER[j].index((c, T - 1))


def plan_products():
    at = {}
    for j in range(1, NB):
        n = T * (NB - j)
        steps = range((j - 1) * TPB, (j - 1) * TPB + 25)
        where = [s for s in steps if not tile(s)[3]]
        more = [s for s in steps if tile(s)[3]]
        lack = n - len(where)
        if lack > 0:
            where = sorted(where + [more[q * len(more) // lack] if more else steps[-1] for q in range(lack)])
        made = [0, 0]
        for q in range(n):
            c, t = j + q // T, q % T
            u = CHUNK_NO[j, c]
            step = where[q * len(where) // n]
            if BEFORE[u] is not None:
                step = max(step, last_use(BEFORE[u]) + 1 + (t // 2 if j == 1 else t))
            at[j, c, t] = min(max(step, made[-1], made[-2] + 1), j * TPB - 1)
            made.append(at[j, c, t])
    return at


PRODUCT_STEP = plan_products()
PRODUCTS_AT = [[x for x in PRODUCTS if PRODUCT_STEP.get(x) == s] for s in range(TILES)]
TAKE_STEP = {x: max(s, min(s + 1, x[0] * TPB - 3)) for x, s in PRODUCT_STEP.items()}
TAKES_AT = [[x for x in PRODUCTS if TAKE_STEP.get(x) == s] for s in range(TILES)]
COLS_STEP = {j: max(TAKE_STEP[x] for x in PRODUCTS if x[0] == j) for j in range(1, NB)}
MERGE_STEP = {j: COLS_STEP[j] + (1 if j > 1 else 0) for j in range(1, NB)}
ROWS_STEP = {j: MERGE_STEP[j] + 1 for j in range(1, NB)}


FIRST_EXP = -5


def plan_exps():
    at = {}
    for j, c in CHUNKS:
        if turned_self(j, c):
            continue
        merged = MERGE_STEP[j] + 2 if j else 0
        for t in range(T):
            step = j * TPB + ORDER[j].index((c, 0)) - 7 + t
            at[j, c, t] = max(step, min(merged, j * TPB - LAG - 1)) if j else max(step, FIRST_EXP)
    return at


EXP_STEP = plan_exps()
assert all(s < j * TPB - LAG for j, s in MERGE_STEP.items())
EXPS_AT = {s: [x for x in PRODUCTS if EXP_STEP.get(x) == s] for s in range(FIRST_EXP, TILES)}
EXP_NO = {x: n for n, x in enumerate(x for s in range(FIRST_EXP, TILES) for x in EXPS_AT[s])}
NEXP = len(EXP_NO)
LAST_EXP = {j: max(EXP_NO[x] for x in EXP_NO if x[0] == j) for j in range(NB)}

SPILLS = {k: [u for u, (j, c) in enumerate(CHUNKS) if c > j and SLOT[u] == k] for k in range(SLOTS)}
LAST_IN_SLOT = {k: max(u for u in range(len(CHUNKS)) if SLOT[u] == k) for k in range(SLOTS)}
X_AT = (NB - 2) * TPB
STATS_AT = X_AT + 8
GROUP_AT = STATS_AT + NB
XN_AT = GROUP_AT + 4
NEXT_AT = XN_AT + 4
NEXT_PRODUCTS = {NEXT_AT + q: x for q, x in enumerate(PRODUCTS[:T * NB])}
assert max(NEXT_PRODUCTS) + 1 < TILES + FIRST_EXP
SPARE_FROM, SPARE_TO = last_use(LAST_IN_SLOT[0]) + 1, NEXT_AT


def plan_buffers():
    free = [0] * LBUFS + [SPARE_FROM] * T
    held = [None] * (LBUFS + T)
    buf, before, step = [], [], []
    for w, p in enumerate(LEFT):
        if turned_self(*tile(p)[:2]):
            buf.append(None)
            before.append(None)
            step.append(None)
            continue
        spare = p - 9 >= SPARE_FROM and p < SPARE_TO
        k = min(range(LBUFS + (T if spare else 0)), key=lambda k: (free[k], k))
        buf.append(k)
        before.append(held[k])
        step.append(max(p - 9, free[k]))
        held[k] = w
        free[k] = p + (-1 if w >= NADD else 2)
    return buf, before, step


LEFT_BUF, LEFT_BEFORE, LOAD_STEP = plan_buffers()
LOADS = {k: [w for w in range(NLEFT) if LEFT_BUF[w] == k] for k in range(LBUFS + T)}
SLOT_USE = [last_use(LAST_IN_SLOT[k]) for k in range(SLOTS)]
SLOT_USE[0] = max(LEFT[w] for w in range(NLEFT) if LEFT_BUF[w] is not None and LEFT_BUF[w] >= LBUFS)
assert all(EXP_STEP[tile(LEFT[w])[1], tile(LEFT[w])[0], 0] < LEFT[LEFT_BEFORE[w]] - LAG
           for w in range(NLEFT) if LEFT_BEFORE[w] is not None)
SPILLS_AT = {}
for _u, (_j, _c) in enumerate(CHUNKS):
    if _c > _j:
        SPILLS_AT.setdefault(TAKE_STEP.get((_j, _c, T - 1), -1), []).append(_u)
INVERT_AT, TAKE_AT, SCALE_AT, WY_AT = 0, 1, 2, (5, 9)
LATE = [int(j + 1 not in PE_SUMS) for j in range(NB)]
G_AT = {T * (c - 1) - 1: c for c in range(2, NB)}
NEXT_G_AT = {TILES - 16 + 4 * c: c for c in range(2)}
assert all(s > p for s, c in NEXT_G_AT.items() for p in range(TILES) if tile(p)[1] <= c)
MAXROW_AT = {min(max(ROWS_STEP[j] + 2, LEFT[LEFT_OF[j - 1][-1]] - 1 if j > 1 else 0), LEFT[LEFT_OF[j][0]] - LAG - 1): j
             for j in range(1, NB)}
AHEAD = {s: min(w for w, p in enumerate(LEFT) if p > s + 6) for s in range(GROUP_AT + 2, max(NEXT_G_AT) + 1)}
FQ = 4
FW = N // FQ
PIECES = [(b, q) for b in range(B) for q in range(FQ)]
FIN_AT = {X_AT + 2 + 3 * q: (True, 2, q) for q in range(FQ)}
LAST_PRODUCT = max(max(PRODUCT_STEP.values()), SLOT_USE[0], SLOT_USE[1])
FIN_ORDER = [(True, q // FQ, q % FQ) for q in range(2 * FQ)] + [(False, q // FQ, q % FQ) for q in range(2 * FQ)]
FIN_AT |= {LAST_PRODUCT + 2 + 5 * n // 2: piece for n, piece in enumerate(FIN_ORDER)}
assert min(s for s, piece in FIN_AT.items() if piece[:2] == (False, 1)) > max(SLOT_USE[2], SLOT_USE[3]) + 1
assert max(FIN_AT) < TILES


def plan_shared(more):
    order = []
    for s in list(range(HEAD, TILES)) + list(range(HEAD)):
        jj, i = divmod(s, TPB)
        body = s >= HEAD
        if s in G_AT and (body or more):
            order.append((int(not body), "g", 0, G_AT[s]))
        if more and s in NEXT_G_AT:
            order.append((1, "g", 0, NEXT_G_AT[s]))
        if i in WY_AT:
            order.append((0, "wy", jj - 1 if body else NB - 1, WY_AT.index(i)))
        if body and jj + 1 < NB and s == COLS_STEP[jj + 1]:
            order.append((0, "cols", jj + 1, 0))
        if body and jj + 1 < NB and s == ROWS_STEP[jj + 1]:
            order.append((0, "rows", jj + 1, 0))
        if more and s - GROUP_AT in (0, 1):
            order.append((1, "gn", 0, s - GROUP_AT))
    return order


SHARED = {more: plan_shared(more) for more in (False, True)}
LAST_HEAD_G = max(c for s, c in G_AT.items() if s < HEAD)


def nonlocal_block(nc, x, wg, bg, ww, vec, out):
    spill = nc.dram_tensor("spill", [PAIRS, P, T, W], F32, kind="Internal").ap()
    yd = nc.dram_tensor("yd", [B, CI, N], F32, kind="Internal").ap()
    xd = x.rearrange("b (k p) n -> b p k n", p=P)
    outd = out.rearrange("b (k p) n -> b p k n", p=P)

    with ExitStack() as ctx:
        def sb(name, shape, dt=F32):
            return ctx.enter_context(nc.sbuf_tensor(name, shape, dt))

        def psum(name, shape):
            return ctx.enter_context(nc.psum_tensor(name, shape, F32))

        def sem(name):
            return ctx.enter_context(nc.semaphore(name))

        with ExitStack() as scope:
            def scoped(name, shape):
                return scope.enter_context(nc.sbuf_tensor(name, shape, F32R))

            xh = scoped("xh", [P, K, N])
            xl = scoped("xl", [P, K, N])
            gh = scoped("gh", [P, NB, T, CI])
            gl = scoped("gl", [P, NB, T, CI])
        fx_a = sb("fx_a", [P, K, N])
        fx_b = sb("fx_b", [P, K, N])
        fy_c = sb("fy_c", [P, N])
        fy_d = sb("fy_d", [P, N])
        ring = sb("ring", [P, SLOTS, T, W])
        xraw = ring[:, SLOTS // 2:, :, :].rearrange("p s t w -> p (s t w)").rearrange("p (k n) -> p k n", k=K)
        fx = [fx_a, fx_b, xraw, fx_a]
        fy = [ring[:, 0:2, :, :].rearrange("p s t w -> p (s t w)"),
              ring[:, 2:4, :, :].rearrange("p s t w -> p (s t w)"),
              fy_c, fy_d]
        wraw = ring[:, 0, 0, 0:K * CI].rearrange("p (k c) -> p k c", k=K)
        colmax = sb("colmax", [P, NB - 1, W])
        lbuf = sb("lbuf", [P, LBUFS, W])
        phi = sb("phi", [P, HIS, W], F32R)
        plo = sb("plo", [P, LOS, W], F32R)
        lacc = sb("lacc", [P, W])
        maxrow = sb("maxrow", [P, W])
        yn = sb("yn", [P, W])
        ident = sb("ident", [P, P])
        gavg = sb("gavg", [P, P])
        ones = sb("ones", [P, 2])
        onesr = sb("onesr", [P, P], F32R)
        wgh = sb("wgh", [P, K, CI], F32R)
        wgl = sb("wgl", [P, K, CI], F32R)
        wwt = sb("wwt", [P, C])
        bgb = sb("bgb", [P, CI])
        vecs = sb("vecs", [P, 3, K])
        bst = sb("bst", [P, K, NB, 6])
        mv = sb("mv", [P, K, 2])
        gst = sb("gst", [P, 4, K])
        neghalf = sb("neghalf", [P, K])
        gnp = sb("gnp", [P, B, 2, K])
        rowm = sb("rowm", [P, T, NB])
        mx = sb("mx", [P, 2, T])
        rmax = sb("rmax", [P, 2, T])
        nmax = sb("nmax", [P, 2, T])
        rsum = sb("rsum", [P, 2, T, NB])
        lsum = sb("lsum", [P, T])
        linv = sb("linv", [P, T])
        bns = sb("bns", [P, K, B * NB, 6])
        bnmv = sb("bnmv", [P, K, 2])
        bnp = sb("bnp", [P, 4, K])
        shift = sb("shift", [P, B, K])

        bank = psum("bank", [P, 8, W])
        fps = bank[:, 0:2, :]
        pps = bank[:, 2:4, :]
        yps = bank[:, 4:6, :]
        lps = bank[:, 6, :]
        sps = bank[:, 7, :]

        consts_in = sem("consts_in")
        consts_made = sem("consts_made")
        zeroed = sem("zeroed")
        wg_hi = sem("wg_hi")
        wg_lo = sem("wg_lo")
        x_in = [sem(f"x_in{q}") for q in range(K * X_CUTS)]
        counted = sem("counted")
        gn_own = sem("gn_own")
        gn_in = sem("gn_in")
        gn_avg = sem("gn_avg")
        gn_var = sem("gn_var")
        gn_rstd = sem("gn_rstd")
        gnp_made = sem("gnp_made")
        xn_made = sem("xn_made")
        xh_made = sem("xh_made")
        xl_made = sem("xl_made")
        g_made = sem("g_made")
        g_added = sem("g_added")
        gh_made = sem("gh_made")
        gl_made = sem("gl_made")
        f_made = sem("f_made")
        f_taken = sem("f_taken")
        cols_made = sem("cols_made")
        max_own = sem("max_own")
        max_made = sem("max_made")
        rows_made = sem("rows_made")
        maxrow_made = sem("maxrow_made")
        spilled = [sem(f"spilled{k}") for k in range(SLOTS)]
        loaded = [sem(f"loaded{k}") for k in range(LBUFS + T)]
        left_sub = sem("left_sub")
        left_exp = sem("left_exp")
        right_exp = sem("right_exp")
        turned = sem("turned")
        hi_made = sem("hi_made")
        lo_made = sem("lo_made")
        left_added = sem("left_added")
        tile_used = sem("tile_used")
        right_summed = sem("right_summed")
        row_taken = sem("row_taken")
        left_summed = sem("left_summed")
        summed = sem("summed")
        inverted = sem("inverted")
        inverse_spread = sem("inverse_spread")
        inverse_taken = sem("inverse_taken")
        y_made = sem("y_made")
        y_stored = sem("y_stored")
        wy_made = sem("wy_made")
        wy_counted = sem("wy_counted")
        bn_own = sem("bn_own")
        bn_var = sem("bn_var")
        bn_rstd = sem("bn_rstd")
        bn_ready = sem("bn_ready")
        fin_x = [sem(f"fin_x{b}") for b in range(B - 1)]
        fin_x_last = [sem(f"fin_x_last{q}") for q in range(FQ)]
        fin_y = [sem(f"fin_y{b}") for b in range(B)]
        fin_wy = sem("fin_wy")
        fin_scaled = sem("fin_scaled")
        fin_added = sem("fin_added")
        fin_out_first = [sem(f"fin_out_first{q}") for q in range(FQ)]
        fin_out = sem("fin_out")

        block = ctx.enter_context(nc.Block())

        def spill_count(n, u):
            mine = SPILLS[SLOT[u]]
            return n * (16 * len(mine)) + 16 * (mine.index(u) + 1)

        def left_at(w):
            j, c, row, _ = tile(LEFT[w])
            if turned_self(j, c):
                return ring[:, SLOT[CHUNK_NO[j, c]], row, :]
            k = LEFT_BUF[w]
            return lbuf[:, k, :] if k < LBUFS else ring[:, 0, k - LBUFS, :]

        def whole(p):
            return pps[:, PSUM_NO[p] % 2, :] if p in PSUM_NO else left_at(LEFT_NO[p])

        @block.sync
        def _(sp):
            def load_x(n, q):
                k, cut = divmod(q, X_CUTS)
                cols = slice(cut * (N // X_CUTS), (cut + 1) * (N // X_CUTS))
                sp.dma_start(xraw[:, k, cols], xd[bass.ds(n, 1), :, k, cols].rearrange("b p n -> p (b n)")
                             ).then_inc(x_in[q], 16)

            def send(n, u):
                sp.wait_ge(f_taken, n * NPROD + PRODUCT_NO[(*CHUNKS[u], T - 1)] + 1)
                sp.dma_start(spill[pair(*CHUNKS[u])], ring[:, SLOT[u], :, :]).then_inc(spilled[SLOT[u]], 16)

            def load_left(b, w):
                j, i, r, _ = tile(LEFT[w])
                v = LEFT_BEFORE[w]
                if v is None and LEFT_BUF[w] < LBUFS:
                    sp.wait_ge(spilled[SLOT[CHUNK_NO[i, j]]], spill_count(b, CHUNK_NO[i, j]))
                elif v is None:
                    sp.wait_ge(tile_used, b * TILES + SPARE_FROM)
                elif v < NADD:
                    sp.wait_ge(left_added, b * NADD + v + 1)
                else:
                    sp.wait_ge(left_exp, b * NLEFT + v + 1)
                sp.dma_start(left_at(w), spill[pair(i, j), :, r, :]).then_inc(loaded[LEFT_BUF[w]], 16)

            def store_y(b, j):
                sp.wait_ge(y_made, b * NB + j + 1)
                sp.dma_start(yd[bass.ds(b, 1), :, j * W:(j + 1) * W].rearrange("b p w -> p (b w)"), yn[:, :]
                             ).then_inc(y_stored, 16)

            def load_final(is_x, b, q):
                cols = slice(q * FW, (q + 1) * FW)
                if is_x:
                    sp.dma_start(fx[b][:, :, cols], xd[b, :, :, cols]
                                 ).then_inc(fin_x[b] if b < B - 1 else fin_x_last[q], 16)
                else:
                    sp.dma_start(fy[b][:, cols], yd[b, :, cols]).then_inc(fin_y[b], 16)

            def step(b, s, more, tail=False):
                if more and s == X_AT:
                    sp.wait_ge(tile_used, b * TILES + max(SLOT_USE[k] for k in range(SLOTS // 2, SLOTS)) + 1)
                    for q in range(K * X_CUTS):
                        load_x(b + 1, q)
                for w in range(NLEFT):
                    if LOAD_STEP[w] == s:
                        load_left(b, w)
                for u in SPILLS_AT.get(s, []):
                    send(b, u)
                if more and s - 1 in NEXT_PRODUCTS:
                    j, c, t = NEXT_PRODUCTS[s - 1]
                    if c > j and t == T - 1:
                        send(b + 1, CHUNK_NO[j, c])
                j, i = divmod(s, TPB)
                if j >= 1 and i == SCALE_AT + LATE[j - 1] + 1:
                    store_y(b, j - 1)
                if tail and s == SCALE_AT + LATE[NB - 1] + 1:
                    store_y(b - 1, NB - 1)
                if not more and s in FIN_AT:
                    is_x, n, q = FIN_AT[s]
                    if q == 0:
                        use = {(True, 2): SLOT_USE[4:8], (False, 0): SLOT_USE[0:2], (False, 1): SLOT_USE[2:4]}
                        if (is_x, n) in use:
                            sp.wait_ge(tile_used, b * TILES + max(use[is_x, n]) + 1)
                        if is_x and n == 0:
                            sp.wait_ge(f_made, B * NPROD)
                        if not is_x and n == 0:
                            sp.wait_ge(y_stored, (B - 1) * (16 * NB))
                    load_final(is_x, n, q)

            for q in range(K * X_CUTS):
                load_x(0, q)
            sp.dma_start(wraw, wg.rearrange("(k p) c -> p k c", p=P)).then_inc(consts_in, 16)
            sp.dma_start(wwt[:, :], ww).then_inc(consts_in, 16)
            sp.dma_start(bgb[:, :], bg.partition_broadcast(P)).then_inc(consts_in, 16)
            sp.dma_start(vecs[:, :, :], vec).then_inc(consts_in, 16)
            for u in SPILLS_AT[-1]:
                send(0, u)
            for s in range(HEAD):
                step(0, s, True)
            with sp.Fori(0, B - 1) as b:
                for s in range(HEAD, TILES):
                    step(b, s, True)
                for s in range(HEAD):
                    step(b + 1, s, True, tail=True)
            for s in range(HEAD, TILES):
                step(B - 1, s, False)
            store_y(B - 1, NB - 1)
            sp.wait_ge(tile_used, B * TILES)
            for q in range(FQ):
                load_final(False, 2, q)
            sp.wait_ge(y_stored, 16 * B * NB)
            for q in range(FQ):
                load_final(False, 3, q)
            for f, (b, q) in enumerate(PIECES):
                cols = slice(q * FW, (q + 1) * FW)
                sp.wait_ge(fin_added, f + 1)
                sp.dma_start(outd[b, :, :, cols], fx[b][:, :, cols]
                             ).then_inc(fin_out if b > 0 else fin_out_first[q], 16)
                if b == 1:
                    sp.wait_ge(fin_out_first[q], 16)
                    load_final(True, B - 1, q)
            sp.wait_ge(fin_out, 16 * (B - 1) * FQ)

        @block.gpsimd
        def _(pool):
            def rstd(n):
                pool.wait_ge(gn_var, n + 1)
                nc.gpsimd.tensor_tensor(gst[:, 3, :], gst[:, 2, :], neghalf[:, :], ALU.pow).then_inc(gn_rstd, 1)

            def make_xl(n, c):
                cols = slice(c * W, (c + 1) * W)
                pool.wait_ge(xh_made, n * NB + c + 1)
                nc.gpsimd.tensor_tensor(xl[:, :, cols], xraw[:, :, cols], xh[:, :, cols].bitcast(F32),
                                        ALU.subtract).then_inc(xl_made, 1)

            def make_gl(b, c):
                pool.wait_ge(gh_made, b * NB + c + 1)
                nc.gpsimd.tensor_tensor(gl[:, c, :, :], lacc[:, :].rearrange("p (t c) -> p t c", t=T),
                                        gh[:, c, :, :].bitcast(F32), ALU.subtract).then_inc(gl_made, 1)

            def image(b, more):
                for c in range(len(NEXT_G_AT), NB):
                    make_gl(b, c)
                for w in range(NLEFT):
                    if more and w == AHEAD[GROUP_AT + 2]:
                        rstd(b + 1)
                    for c in range(NB):
                        if more and w == AHEAD[XN_AT + c]:
                            make_xl(b + 1, c)
                    for s, c in NEXT_G_AT.items():
                        if more and w == AHEAD[s]:
                            make_gl(b + 1, c)
                    j = tile(LEFT[w])[0]
                    if w == LEFT_OF[j][0]:
                        pool.wait_ge(maxrow_made, b * (NB - 1) + j)
                    if LEFT_BUF[w] is not None:
                        mine = LOADS[LEFT_BUF[w]]
                        pool.wait_ge(loaded[LEFT_BUF[w]], b * (16 * len(mine)) + 16 * (mine.index(w) + 1))
                    nc.gpsimd.tensor_tensor(left_at(w), left_at(w), maxrow[:, :],
                                            ALU.subtract).then_inc(left_sub, 1)

            nc.gpsimd.memset(neghalf[:, :], -0.5)
            nc.gpsimd.memset(ones[:, :], 1.0)
            nc.gpsimd.memset(onesr[:, :].bitcast(F32), 1.0)
            nc.gpsimd.memset(ident[:, :], 0.0)
            nc.gpsimd.memset(gavg[:, :], 1.0 / GROUP).then_inc(zeroed, 1)
            pool.wait_ge(zeroed, 1)
            nc.gpsimd.affine_select(out=ident[:, :], in_=ident[:, :], compare_op=ALU.not_equal, fill=1.0, base=0,
                                    pattern=[[-1, P]], channel_multiplier=1)
            gv = gavg[:, :].rearrange("p (g c) -> p g c", c=GROUP)
            nc.gpsimd.affine_select(out=gv, in_=gv, compare_op=ALU.is_ge, fill=0.0, base=0,
                                    pattern=[[-GROUP, P // GROUP], [0, GROUP]], channel_multiplier=1).then_inc(zeroed, 1)
            pool.wait_ge(zeroed, 2)
            nc.gpsimd.affine_select(out=gv, in_=gv, compare_op=ALU.is_ge, fill=0.0, base=GROUP - 1,
                                    pattern=[[GROUP, P // GROUP], [0, GROUP]], channel_multiplier=-1
                                    ).then_inc(consts_made, 1)
            rstd(0)
            for c in range(NB):
                make_xl(0, c)
            for c in NEXT_G_AT.values():
                make_gl(0, c)
            with pool.Fori(0, B - 1) as b:
                image(b, True)
            image(B - 1, False)
            pool.wait_ge(bn_var, 1)
            nc.gpsimd.tensor_tensor(bnp[:, 0, :], bnp[:, 0, :], neghalf[:, :], ALU.pow).then_inc(bn_rstd, 1)

        @block.scalar
        def _(act):
            def make_xh(n, c):
                act.wait_ge(xn_made, n * NB + c + 1)
                nc.scalar.copy(xh[:, :, c * W:(c + 1) * W], xraw[:, :, c * W:(c + 1) * W]).then_inc(xh_made, 1)

            def make_gh(b, c, first=False):
                if c in NEXT_G_AT.values() and not first:
                    act.wait_ge(tile_used, (b - 1) * TILES + max(p for p in range(TILES) if tile(p)[1] == c) + 1)
                act.wait_ge(g_added, b * NB + c + 1)
                nc.scalar.copy(gh[:, c, :, :], lacc[:, :].rearrange("p (t c) -> p t c", t=T)).then_inc(gh_made, 1)

            def exp_right(b, j, c, t):
                u = CHUNK_NO[j, c]
                if t == 0:
                    act.wait_ge(max_made, b * NB + j + 1)
                    if c > j:
                        act.wait_ge(spilled[SLOT[u]], spill_count(b, u))
                nc.scalar.activation(ring[:, SLOT[u], t, :], ring[:, SLOT[u], t, :], ACT.Exp,
                                     bias=nmax[:, j % 2, t:t + 1], accum_out=rsum[:, j % 2, t, c:c + 1]
                                     ).then_inc(right_exp, 1)

            def take_maxrow(b, j):
                act.wait_ge(rows_made, b * (NB - 1) + j)
                if j > 1:
                    act.wait_ge(left_sub, b * NLEFT + LEFT_OF[j][0])
                nc.scalar.copy(maxrow[:, :], sps).then_inc(maxrow_made, 1)

            def exp_left(b, p):
                w = LEFT_NO[p]
                act.wait_ge(left_sub, b * NLEFT + w + 1)
                if p in PSUM_NO:
                    act.wait_ge(lo_made, b * TILES + IN_PSUM[PSUM_NO[p] - 2] + 1)
                nc.scalar.activation(whole(p), left_at(w), ACT.Exp).then_inc(left_exp, 1)

            def split_hi(b, p, first=False):
                if tile(p)[3]:
                    act.wait_ge(left_exp, b * NLEFT + LEFT_NO[p] + 1)
                else:
                    act.wait_ge(turned, b * (TILES - NLEFT) + RIGHT_NO[p] + 1)
                if HI_BEFORE[p] >= 0 or not first:
                    act.wait_ge(tile_used, b * TILES + HI_BEFORE[p] + 1)
                nc.scalar.copy(phi[:, HI_BUF[p], :], whole(p)).then_inc(hi_made, 1)

            def take_sums(b, j):
                act.wait_ge(tile_used, b * TILES + LEFT[LEFT_OF[j][-1]] + 1)
                nc.scalar.copy(lacc[0:1, :], lps[0:1, :]).then_inc(row_taken, 1)

            def take_inverse(b, j):
                act.wait_ge(inverse_spread, b * NB + j + 1)
                if j > 0:
                    act.wait_ge(wy_made, b * (K * NB) + K * j)
                    act.wait_ge(y_stored, b * (16 * NB) + 16 * j)
                nc.scalar.copy(yn[:, :], lps).then_inc(inverse_taken, 1)

            def step(b, s, more, tail=False, first=False):
                j, i = divmod(s, TPB)
                if tail and s == 0:
                    take_sums(b - 1, NB - 1)
                if tail and s == TAKE_AT + 1:
                    take_inverse(b - 1, NB - 1)
                if tail and s == HEAD - 1:
                    act.wait_ge(wy_made, b * (K * NB))
                    act.wait_ge(y_stored, b * (16 * NB))
                if s in MAXROW_AT:
                    take_maxrow(b, MAXROW_AT[s])
                if s + LAG + 1 in LEFT_NO and s + LAG + 1 not in PSUM_NO:
                    exp_left(b, s + LAG + 1)
                if s + LAG in LEFT_NO and s + LAG in PSUM_NO:
                    exp_left(b, s + LAG)
                if s + LAG < TILES:
                    split_hi(b, s + LAG, first)
                elif more:
                    split_hi(b + 1, s + LAG - TILES)
                for x3 in EXPS_AT[s]:
                    exp_right(b, *x3)
                if more and s - TILES in EXPS_AT:
                    for x3 in EXPS_AT[s - TILES]:
                        exp_right(b + 1, *x3)
                if s - 1 in G_AT:
                    make_gh(b, G_AT[s - 1])
                if more and s - 1 in NEXT_G_AT:
                    make_gh(b + 1, NEXT_G_AT[s - 1])
                if j in PE_SUMS and i == TPB - 1 and j < NB - 1:
                    take_sums(b, j)
                if j >= 1 and i == TAKE_AT + LATE[j - 1]:
                    take_inverse(b, j - 1)
                if more and 0 <= s - XN_AT < NB:
                    make_xh(b + 1, s - XN_AT)

            act.wait_ge(consts_in, 16 * 4)
            nc.scalar.copy(wgh[:, :, :], wraw).then_inc(wg_hi, 1)
            for c in range(NB):
                make_xh(0, c)
            for c in NEXT_G_AT.values():
                make_gh(0, c, first=True)
            for s in range(FIRST_EXP, 0):
                for x3 in EXPS_AT[s]:
                    exp_right(0, *x3)
                if s + LAG >= 0:
                    split_hi(0, s + LAG, first=True)
            for s in range(HEAD):
                step(0, s, True, first=True)
            with act.Fori(0, B - 1) as b:
                for s in range(HEAD, TILES):
                    step(b, s, True)
                for s in range(HEAD):
                    step(b + 1, s, True, tail=True)
            for s in range(HEAD, TILES):
                step(B - 1, s, False)
            take_sums(B - 1, NB - 1)
            take_inverse(B - 1, NB - 1)
            act.wait_ge(bn_ready, 1)
            for f, (b, q) in enumerate(PIECES):
                if b == B - 1:
                    act.wait_ge(fin_x_last[q], 16)
                elif q == 0:
                    act.wait_ge(fin_x[b], 16 * FQ)
                for k in range(K):
                    px = fx[b][:, k, q * FW:(q + 1) * FW]
                    last = nc.scalar.activation(px, px, ACT.Identity,
                                                scale=gnp[:, b, 1, k:k + 1], bias=shift[:, b, k:k + 1])
                last.then_inc(fin_scaled, 1)

        @block.vector
        def _(dve):
            def count_x(n, i):
                k, c = divmod(2 * i, NB)
                if c % (NB // X_CUTS) == 0:
                    dve.wait_ge(x_in[k * X_CUTS + c // (NB // X_CUTS)], n * 16 + 16)
                for cc in (c, c + 1):
                    last = nc.vector.bn_stats(bst[:, k, cc, :], xraw[:, k, cc * W:(cc + 1) * W])
                last.then_inc(counted, 1)

            def group(n, stage):
                if stage == 0:
                    dve.wait_ge(counted, n * NB + NB)
                    nc.vector.memset(gst[:, 3, :], 0.0)
                    for k in range(K):
                        last = nc.vector.bn_aggr(mv[:, k, :], bst[:, k, :, :])
                    last.then_inc(gn_in, 1)
                elif stage == 1:
                    dve.wait_ge(gn_avg, n * 2 + 1)
                    nc.vector.tensor_copy(gst[:, 0, :], sps[:, 0:K]).then_inc(gn_own, 1)
                    dve.wait_ge(gn_own, n * 3 + 1)
                    nc.vector.tensor_tensor(gst[:, 1, :], mv[:, :, 0], gst[:, 0, :], ALU.subtract).then_inc(gn_own, 1)
                    dve.wait_ge(gn_own, n * 3 + 2)
                    nc.vector.tensor_tensor(gst[:, 1, :], gst[:, 1, :], gst[:, 1, :], ALU.mult).then_inc(gn_own, 1)
                    dve.wait_ge(gn_own, n * 3 + 3)
                    nc.vector.tensor_tensor(gst[:, 1, :], gst[:, 1, :], mv[:, :, 1], ALU.add).then_inc(gn_in, 1)
                elif stage == 2:
                    dve.wait_ge(gn_avg, n * 2 + 2)
                    nc.vector.tensor_scalar(gst[:, 2, :], sps[:, K:2 * K], GN_EPS, None, ALU.add).then_inc(gn_var, 1)
                else:
                    dve.wait_ge(gn_rstd, n + 1)
                    nc.vector.tensor_tensor(gnp[:, bass.ds(n, 1), 0, :].rearrange("p b k -> p (b k)"), gst[:, 0, :],
                                            gst[:, 3, :], ALU.mult)
                    nc.vector.tensor_scalar(gnp[:, bass.ds(n, 1), 1, :].rearrange("p b k -> p (b k)"), gst[:, 3, :],
                                            1.0, None, ALU.add).then_inc(gnp_made, 1)

            def make_xn(n, c):
                cols = slice(c * W, (c + 1) * W)
                for k in range(K):
                    last = nc.vector.tensor_scalar(xraw[:, k, cols], xraw[:, k, cols], gst[:, 0, k:k + 1],
                                                   gst[:, 3, k:k + 1], ALU.subtract, ALU.mult)
                last.then_inc(xn_made, 1)

            def add_bias(n, c, first=False):
                dve.wait_ge(g_made, n * NB + c + 1)
                if c == len(NEXT_G_AT) and not first:
                    dve.wait_ge(left_summed, n * (NB - 1))
                elif c > 0:
                    dve.wait_ge(gl_made, n * NB + c)
                elif not first:
                    dve.wait_ge(left_summed, n * (NB - 1) - 1)
                nc.vector.tensor_tensor(lacc[:, :].rearrange("p (t c) -> p t c", t=T),
                                        sps.rearrange("p (t c) -> p t c", t=T),
                                        bgb[:, :].unsqueeze(1).broadcast_to([P, T, CI]), ALU.add).then_inc(g_added, 1)

            def take_f(n, j, c, t, before=True):
                s = PRODUCT_NO[j, c, t]
                u = CHUNK_NO[j, c]
                if t == 0:
                    if BEFORE[u] is not None:
                        dve.wait_ge(tile_used, n * TILES + last_use(BEFORE[u]) + 1)
                    else:
                        if before:
                            dve.wait_ge(tile_used, n * TILES + SLOT_USE[u] + 1 - TILES)
                        if u >= SLOTS // 2:
                            dve.wait_ge(xl_made, n * NB + NB)
                dve.wait_ge(f_made, n * NPROD + s + 1)
                src = fps[:, s % 2, :]
                last = nc.vector.tensor_scalar(ring[:, SLOT[u], t, :], src, 1.0, None, ALU.mult, ALU.max,
                                               accum_out=rowm[:, t, c:c + 1])
                if c > j:
                    cm = colmax[:, c - 1, :]
                    if j == 0 and t == 0:
                        last = nc.vector.tensor_copy(cm, src)
                    else:
                        if t > 0:
                            dve.wait_ge(f_taken, n * NPROD + s)
                        last = nc.vector.tensor_tensor(cm, src, cm, ALU.max)
                last.then_inc(f_taken, 1)

            def merge_max(n, j):
                own_max = rmax[:, j % 2, :]
                steps = n * (2 * NB - 1)
                dve.wait_ge(f_taken, n * NPROD + PRODUCT_NO[j, NB - 1, T - 1] + 1)
                if j == 0:
                    nc.vector.tensor_reduce(own_max, rowm[:, :, j:], AX.X, ALU.max).then_inc(max_own, 1)
                    dve.wait_ge(max_own, steps + 1)
                else:
                    nc.vector.tensor_reduce(mx[:, 0, :], rowm[:, :, j:], AX.X, ALU.max)
                    dve.wait_ge(cols_made, n * (NB - 1) + j)
                    nc.vector.tensor_reduce(mx[:, 1, :], sps.rearrange("p (t c) -> p t c", t=T),
                                            AX.X, ALU.max).then_inc(max_own, 1)
                    dve.wait_ge(max_own, steps + 2 * j)
                    nc.vector.tensor_tensor(own_max, mx[:, 0, :], mx[:, 1, :], ALU.max).then_inc(max_own, 1)
                    dve.wait_ge(max_own, steps + 2 * j + 1)
                nc.vector.tensor_scalar(nmax[:, j % 2, :], own_max, -1.0, None, ALU.mult).then_inc(max_made, 1)

            def split_lo(b, p, first=False):
                dve.wait_ge(hi_made, b * TILES + p + 1)
                if p >= LOS or not first:
                    dve.wait_ge(tile_used, b * TILES + p - LOS + 1)
                nc.vector.tensor_tensor(plo[:, p % LOS, :], whole(p), phi[:, HI_BUF[p], :].bitcast(F32),
                                        ALU.subtract).then_inc(lo_made, 1)

            def add_left(b, w):
                if w == LEFT_OF[LEFT[w] // TPB][0]:
                    if w == 0:
                        dve.wait_ge(gl_made, b * NB + NB)
                    else:
                        dve.wait_ge(left_summed, b * (NB - 1) + LEFT[w] // TPB - 1)
                    nc.vector.tensor_copy(lacc[:, :], left_at(w)).then_inc(left_added, 1)
                else:
                    dve.wait_ge(left_added, b * NADD + w)
                    nc.vector.tensor_tensor(lacc[:, :], left_at(w), lacc[:, :], ALU.add).then_inc(left_added, 1)

            def sum_right(b, j):
                dve.wait_ge(right_exp, b * NEXP + LAST_EXP[j] + 1)
                first = j + 1 if turned_self(j, j) else j
                nc.vector.tensor_reduce(lsum[:, :], rsum[:, j % 2, :, first:], AX.X, ALU.add).then_inc(right_summed, 1)

            def invert(b, j):
                dve.wait_ge(right_summed, b * NB + j + 1)
                if j > 0:
                    dve.wait_ge(left_summed, b * (NB - 1) + j)
                    nc.vector.tensor_tensor(lsum[:, :], lps[:, 0:2 * T].rearrange("p (t o) -> p t o", o=2)[:, :, 0],
                                            lsum[:, :], ALU.add).then_inc(summed, 1)
                    dve.wait_ge(summed, b * (NB - 1) + j)
                nc.vector.reciprocal(linv[:, :], lsum[:, :]).then_inc(inverted, 1)

            def scale(b, j):
                dve.wait_ge(inverse_taken, b * NB + j + 1)
                nc.vector.tensor_tensor(yn[:, :], yps[:, j % 2, :], yn[:, :], ALU.mult).then_inc(y_made, 1)

            def count_wy(b, j, h):
                dve.wait_ge(wy_made, b * (K * NB) + K * j + h + 1)
                nc.vector.bn_stats(bns[:, h, bass.ds(b * NB + j, 1), :].rearrange("p n s -> p (n s)"), sps
                                   ).then_inc(wy_counted, 1)

            def step(b, p, more, tail=False, first=False):
                j, i = divmod(p, TPB)
                split_lo(b, p, first)
                for w in ADDS_AT[p]:
                    add_left(b, w)
                if p - 1 in G_AT:
                    add_bias(b, G_AT[p - 1], first)
                if more and p - 1 in NEXT_G_AT:
                    add_bias(b + 1, NEXT_G_AT[p - 1])
                if j >= 1 and i == INVERT_AT + LATE[j - 1]:
                    invert(b, j - 1)
                if more and 0 <= p - GROUP_AT < 4:
                    group(b + 1, p - GROUP_AT)
                for x3 in TAKES_AT[p]:
                    take_f(b, *x3)
                if j + 1 < NB and p == MERGE_STEP[j + 1]:
                    merge_max(b, j + 1)
                if j >= 1 and i == SCALE_AT + LATE[j - 1]:
                    scale(b, j - 1)
                if j >= 1 and i - 1 in WY_AT:
                    count_wy(b, j - 1, WY_AT.index(i - 1))
                if tail and i == INVERT_AT + 1:
                    invert(b - 1, NB - 1)
                if tail and i == SCALE_AT + 1:
                    scale(b - 1, NB - 1)
                if tail and i - 1 in WY_AT:
                    count_wy(b - 1, NB - 1, WY_AT.index(i - 1))
                if more and 0 <= p - STATS_AT < NB:
                    count_x(b + 1, p - STATS_AT)
                if more and 0 <= p - XN_AT < NB:
                    make_xn(b + 1, p - XN_AT)
                if more and p - 1 in NEXT_PRODUCTS:
                    take_f(b + 1, *NEXT_PRODUCTS[p - 1])
                    if p - 1 == max(NEXT_PRODUCTS):
                        merge_max(b + 1, 0)
                if i == TPB - 2:
                    sum_right(b, j)

            for i in range(NB):
                count_x(0, i)
            for stage in range(4):
                group(0, stage)
            dve.wait_ge(wg_hi, 1)
            nc.vector.tensor_tensor(wgl[:, :, :], wraw, wgh[:, :, :].bitcast(F32), ALU.subtract).then_inc(wg_lo, 1)
            for c in range(NB):
                make_xn(0, c)
            for x3 in PRODUCTS[:T * NB]:
                take_f(0, *x3, before=False)
            merge_max(0, 0)
            add_bias(0, 0, first=True)
            add_bias(0, 1, first=True)
            for p in range(HEAD):
                step(0, p, True, first=True)
            with dve.Fori(0, B - 1) as b:
                for p in range(HEAD, TILES):
                    step(b, p, True)
                for p in range(HEAD):
                    step(b + 1, p, True, tail=True)
            for p in range(HEAD, TILES):
                step(B - 1, p, False)
            invert(B - 1, NB - 1)
            scale(B - 1, NB - 1)
            for h in range(K):
                count_wy(B - 1, NB - 1, h)
            dve.wait_ge(wy_counted, B * K * NB)
            for k in range(K):
                last = nc.vector.bn_aggr(bnmv[:, k, :], bns[:, k, :, :])
            last.then_inc(bn_own, 1)
            dve.wait_ge(bn_own, 1)
            nc.vector.tensor_scalar(bnp[:, 0, :], bnmv[:, :, 1], BN_EPS, None, ALU.add).then_inc(bn_var, 1)
            dve.wait_ge(bn_rstd, 1)
            nc.vector.tensor_tensor(bnp[:, 1, :], bnp[:, 0, :], vecs[:, 1, :], ALU.mult)
            nc.vector.tensor_tensor(bnp[:, 2, :], bnmv[:, :, 0], vecs[:, 0, :], ALU.add).then_inc(bn_own, 1)
            dve.wait_ge(bn_own, 2)
            nc.vector.tensor_tensor(bnp[:, 2, :], bnp[:, 2, :], bnp[:, 1, :], ALU.mult)
            nc.vector.tensor_tensor(bnp[:, 3, :], vecs[:, 0, :], bnp[:, 1, :], ALU.mult).then_inc(bn_own, 1)
            dve.wait_ge(bn_own, 3)
            nc.vector.tensor_tensor(bnp[:, 2, :], vecs[:, 2, :], bnp[:, 2, :], ALU.subtract).then_inc(bn_own, 1)
            dve.wait_ge(bn_own, 4)
            nc.vector.tensor_tensor(bnp[:, 3, :], bnp[:, 2, :], bnp[:, 3, :], ALU.add).then_inc(bn_own, 1)
            dve.wait_ge(bn_own, 5)
            for b in range(B):
                last = nc.vector.tensor_tensor(shift[:, b, :], bnp[:, 3, :], gnp[:, b, 0, :], ALU.subtract)
            last.then_inc(bn_ready, 1)
            for f, (b, q) in enumerate(PIECES):
                dve.wait_ge(fin_scaled, f + 1)
                dve.wait_ge(fin_wy, f + 1)
                for k in range(K):
                    px = fx[b][:, k, q * FW:(q + 1) * FW]
                    wy = bank[:, 4 * (f % 2) + 2 * k:4 * (f % 2) + 2 * k + 2, :].rearrange("p a w -> p (a w)")
                    last = nc.vector.scalar_tensor_tensor(out=px, in0=wy, scalar=bnp[:, 1, k:k + 1], in1=px,
                                                          op0=ALU.mult, op1=ALU.add)
                last.then_inc(fin_added, 1)

        @block.tensor
        def _(pe):
            last_image = B - 1

            def average(n, stage, first=False):
                if not first:
                    shared_free(n, "gn", 0, stage)
                pe.wait_ge(gn_in, n * 2 + stage + 1)
                nc.tensor.matmul(sps[:, K * stage:K * (stage + 1)], gavg[:, :], gst[:, 1, :] if stage else mv[:, :, 0],
                                 start=True, stop=True).then_inc(gn_avg, 1)

            def multiply(n, j, c, t, first=False):
                s = PRODUCT_NO[j, c, t]
                if j == 0 and t == 0:
                    pe.wait_ge(xl_made, n * NB + c + 1)
                if s >= 2 or not first:
                    pe.wait_ge(f_taken, n * NPROD + s - 1)
                rows = slice(j * W + t * P, j * W + (t + 1) * P)
                cols = slice(c * W, (c + 1) * W)
                dst = fps[:, s % 2, :]
                for k in range(K):
                    nc.tensor.matmul(dst, xh[:, k, rows], xh[:, k, cols], start=(k == 0), stop=False)
                    nc.tensor.matmul(dst, xh[:, k, rows], xl[:, k, cols], start=False, stop=False)
                    last = nc.tensor.matmul(dst, xl[:, k, rows], xh[:, k, cols], start=False, stop=(k == K - 1))
                last.then_inc(f_made, 1)

            def make_g(b, c, first=False):
                if not first:
                    shared_free(b, "g", 0, c)
                elif c > 0:
                    pe.wait_ge(g_added, c)
                for r in range(T):
                    rows = slice(c * W + r * P, c * W + (r + 1) * P)
                    dst = sps[:, r * CI:(r + 1) * CI]
                    for k in range(K):
                        nc.tensor.matmul(dst, xh[:, k, rows], wgh[:, k, :], start=(k == 0), stop=False)
                        nc.tensor.matmul(dst, xh[:, k, rows], wgl[:, k, :], start=False, stop=False)
                        last = nc.tensor.matmul(dst, xl[:, k, rows], wgh[:, k, :], start=False, stop=(k == K - 1))
                last.then_inc(g_made, 1)

            def turn(b, p, first=False):
                j, c, r, left = tile(p)
                if left:
                    return
                pe.wait_ge(right_exp, b * NEXP + max(EXP_NO[j, c, t] for t in range(T)) + 1)
                n = PSUM_NO[p]
                if n >= 2:
                    pe.wait_ge(lo_made, b * TILES + IN_PSUM[n - 2] + 1)
                elif not first:
                    pe.wait_ge(lo_made, b * TILES + IN_PSUM[n - 2] + 1 - TILES)
                k = SLOT[CHUNK_NO[j, c]]
                for t in range(T):
                    last = nc.tensor.transpose(pps[:, n % 2, t * P:(t + 1) * P],
                                               ring[:, k, t, r * P:(r + 1) * P], ident[:, :])
                last.then_inc(turned, 1)

            def attend(b, p, first=False):
                j, c, r, left = tile(p)
                i = p % TPB
                y = yps[:, j % 2, :]
                if j == 0 and r == 0:
                    pe.wait_ge(gl_made, b * NB + c + 1)
                pe.wait_ge(lo_made, b * TILES + p + 1)
                if i == 0 and j != 1 and not first:
                    pe.wait_ge(y_made, b * NB + j - 1)
                hi, lo = phi[:, HI_BUF[p], :], plo[:, p % LOS, :]
                nc.tensor.matmul(y, gh[:, c, r, :], hi, start=(i == 0), stop=False)
                nc.tensor.matmul(y, gl[:, c, r, :], hi, start=False, stop=False)
                last = nc.tensor.matmul(y, gh[:, c, r, :], lo, start=False, stop=(i == TPB - 1))
                if left and j in PE_SUMS:
                    w = LEFT_NO[p]
                    begin = w == LEFT_OF[j][0]
                    if begin:
                        pe.wait_ge(inverse_taken, b * NB + j)
                    nc.tensor.matmul(lps, onesr[:, :], hi, start=begin, stop=False)
                    last = nc.tensor.matmul(lps, onesr[:, :], lo, start=False, stop=(w == LEFT_OF[j][-1]))
                last.then_inc(tile_used, 1)

            def shared_free(n, kind, j, h=0):
                order = SHARED[not isinstance(n, int)]
                at = next(q for q, use in enumerate(order) if use[1:] == (kind, j, h))
                image = n - order[at][0]
                ahead, kind, j, h = order[at - 1] if at else (0, "g", 0, LAST_HEAD_G)
                n = image + ahead
                if kind == "g":
                    pe.wait_ge(g_added, n * NB + h + 1)
                elif kind == "cols":
                    pe.wait_ge(max_made, n * NB + j + 1)
                elif kind == "rows":
                    pe.wait_ge(maxrow_made, n * (NB - 1) + j)
                elif kind == "gn" and h == 0:
                    pe.wait_ge(gn_own, n * 3 + 1)
                elif kind == "gn":
                    pe.wait_ge(gn_var, n + 1)
                elif kind == "wy":
                    pe.wait_ge(wy_counted, n * (K * NB) + K * j + h + 1)

            def turn_cols(b, j):
                shared_free(b, "cols", j)
                pe.wait_ge(f_taken, b * NPROD + PRODUCT_NO[j - 1, j, T - 1] + 1)
                for t in range(T):
                    last = nc.tensor.transpose(sps[:, t * P:(t + 1) * P], colmax[:, j - 1, t * P:(t + 1) * P],
                                               ident[:, :])
                last.then_inc(cols_made, 1)

            def spread_rows(b, j):
                shared_free(b, "rows", j)
                for t in range(T):
                    last = nc.tensor.matmul(sps[:, t * P:(t + 1) * P], rmax[:, j % 2, t:t + 1].broadcast_to([P, P]),
                                            ident[:, :], start=True, stop=True)
                last.then_inc(rows_made, 1)

            def sum_left(b, j):
                if j in PE_SUMS:
                    pe.wait_ge(row_taken, b * len(PE_SUMS) + PE_SUMS.index(j) + 1)
                    src, one = lacc[0:1, :], ones[0:1, :]
                else:
                    pe.wait_ge(left_added, b * NADD + LEFT_OF[j][-1] + 1)
                    pe.wait_ge(inverse_taken, b * NB + j)
                    src, one = lacc[:, :], ones[:, :]
                for t in range(T):
                    last = nc.tensor.matmul(lps[:, 2 * t:2 * t + 2], src[:, t * P:(t + 1) * P], one,
                                            start=True, stop=True)
                last.then_inc(left_summed, 1)

            def spread_inverse(b, j):
                pe.wait_ge(inverted, b * NB + j + 1)
                for t in range(T):
                    last = nc.tensor.matmul(lps[:, t * P:(t + 1) * P], linv[:, t:t + 1].broadcast_to([P, P]),
                                            ident[:, :], start=True, stop=True)
                last.then_inc(inverse_spread, 1)

            def project(b, j, h):
                pe.wait_ge(y_made, b * NB + j + 1)
                shared_free(b, "wy", j, h)
                nc.tensor.matmul(sps, wwt[:, h * P:(h + 1) * P], yn[:, :], start=True, stop=True
                                 ).then_inc(wy_made, 1)

            def step(b, p, more, tail=False, first=False):
                j, i = divmod(p, TPB)
                if p + LAG < TILES:
                    turn(b, p + LAG, first)
                elif more:
                    turn(b + 1, p + LAG - TILES)
                for x3 in PRODUCTS_AT[p]:
                    multiply(b, *x3)
                if more and p in NEXT_PRODUCTS:
                    multiply(b + 1, *NEXT_PRODUCTS[p])
                attend(b, p, first)
                if 0 < j < NB - 1 and i == TPB - 1:
                    sum_left(b, j)
                if tail and i == INVERT_AT:
                    sum_left(b - 1, NB - 1)
                if tail and i == INVERT_AT + 1:
                    spread_inverse(b - 1, NB - 1)
                if j >= 1 and i == INVERT_AT + LATE[j - 1]:
                    spread_inverse(b, j - 1)
                if p in G_AT:
                    make_g(b, G_AT[p], first)
                if more and p in NEXT_G_AT:
                    make_g(b + 1, NEXT_G_AT[p])
                if j >= 1 and i in WY_AT:
                    project(b, j - 1, WY_AT.index(i))
                if tail and i in WY_AT:
                    project(b - 1, NB - 1, WY_AT.index(i))
                if j + 1 < NB and p == COLS_STEP[j + 1]:
                    turn_cols(b, j + 1)
                if j + 1 < NB and p == ROWS_STEP[j + 1]:
                    spread_rows(b, j + 1)
                if more and p - GROUP_AT in (0, 1):
                    average(b + 1, p - GROUP_AT)

            pe.wait_ge(consts_made, 1)
            for stage in range(2):
                average(0, stage, first=True)
            for x3 in PRODUCTS[:T * NB]:
                multiply(0, *x3, first=True)
            pe.wait_ge(wg_lo, 1)
            for c in NEXT_G_AT.values():
                make_g(0, c, first=True)
            for p in range(LAG):
                turn(0, p, first=True)
            for p in range(HEAD):
                step(0, p, True, first=True)
            with pe.Fori(0, B - 1) as b:
                for p in range(HEAD, TILES):
                    step(b, p, True)
                for p in range(HEAD):
                    step(b + 1, p, True, tail=True)
            for p in range(HEAD, TILES):
                step(last_image, p, False)
            sum_left(last_image, NB - 1)
            spread_inverse(last_image, NB - 1)
            for h in range(K):
                project(last_image, NB - 1, h)
            for f, (b, q) in enumerate(PIECES):
                if f == 0:
                    pe.wait_ge(wy_counted, B * K * NB)
                if f >= 2:
                    pe.wait_ge(fin_added, f - 1)
                if q == 0:
                    pe.wait_ge(fin_y[b], 16 * FQ)
                for k in range(K):
                    for h in range(FW // W):
                        last = nc.tensor.matmul(bank[:, 4 * (f % 2) + 2 * k + h, :], wwt[:, k * P:(k + 1) * P],
                                                fy[b][:, q * FW + h * W:q * FW + (h + 1) * W], start=True, stop=True)
                last.then_inc(fin_wy, 1)


_INS = ("x", "wg", "bg", "ww", "vec")


def kernel(x, L0_conv_g_w, L0_conv_g_b, L0_conv_W_w, L0_conv_W_b, L0_conv_gamma, L0_conv_beta):
    import numpy as np
    import concourse.bacc as bacc
    from concourse.bass_utils import run_bass_kernel_spmd

    nc = bacc.Bacc("TRN2", target_bir_lowering=False, num_devices=1)
    shape = np.shape(x)
    given = dict(
        x=np.ascontiguousarray(x).reshape(B, C, N),
        wg=np.ascontiguousarray(np.transpose(L0_conv_g_w)),
        bg=np.ascontiguousarray(L0_conv_g_b),
        ww=np.ascontiguousarray(np.transpose(L0_conv_W_w)),
        vec=np.ascontiguousarray(np.transpose(np.reshape(
            np.stack([L0_conv_W_b, L0_conv_gamma, L0_conv_beta]), (3, K, P)), (2, 0, 1))),
    )
    args = [nc.dram_tensor(f"{n}_dram", given[n].shape, F32, kind="ExternalInput").ap() for n in _INS]
    out = nc.dram_tensor("out_dram", (B, C, N), F32, kind="ExternalOutput").ap()
    nonlocal_block(nc, *args, out)
    r = run_bass_kernel_spmd(nc, [{f"{n}_dram": given[n] for n in _INS}], core_ids=[0])
    return r.results[0]["out_dram"].reshape(shape)
```
